# Optimizing a Trainium2 kernel written in Bass

```python
import numpy as np
import jax
import jax.numpy as jnp

def _softmax(x, axis=-1):
    return jax.nn.softmax(x, axis=axis)

def _gelu(x):
    return jax.nn.gelu(x, approximate=True)

def _silu(x):
    return jax.nn.silu(x)

def _sigmoid(x):
    return jax.nn.sigmoid(x)

def _layernorm(x, axis=-1, eps=1e-05):
    m = jnp.mean(x, axis=axis, keepdims=True)
    v = jnp.var(x, axis=axis, keepdims=True)
    return (x - m) / jnp.sqrt(v + eps)

def _scatter_add(tgt, idx, src, axis=0):
    return tgt.at[idx].add(src)

def _segment_sum(src, seg, n):
    return jax.ops.segment_sum(src, seg, n)
kernel_name = 'mk_metaformer_d1_conv_nhwc768_r4_6bacf0'

def setup_inputs(seed: int=0):
    np.random.seed(seed)
    _w = jnp.asarray

    def _rec_inputs():
        import jax
        import jax.numpy as jnp
        _gk = jax.random.key(seed)
        x = -0.0005963 + 1.001 * jax.random.normal(jax.random.fold_in(_gk, 1), (4, 32, 32, 192), jnp.float32)
        return x
    x = _rec_inputs()

    def _L0_conv_setup():
        import jax, jax.numpy as jnp
        import numpy as np
        B, H, W, DIM, HEADS = (4, 32, 32, 192, 12)
        HD = DIM // HEADS
        key = jax.random.key(seed)
        ks = jax.random.split(key, 5)
        return {'x': jax.random.normal(ks[0], (B, H, W, DIM), jnp.float32), 'qkv_w': jax.random.normal(ks[1], (3 * DIM, DIM), jnp.float32) * 0.02, 'qkv_b': jnp.zeros((3 * DIM,), jnp.float32), 'proj_w': jax.random.normal(ks[2], (DIM, DIM), jnp.float32) * 0.02, 'proj_b': jnp.zeros((DIM,), jnp.float32), 'rel_pos_h': jax.random.normal(ks[3], (2 * H - 1, HD), jnp.float32) * 0.02, 'rel_pos_w': jax.random.normal(ks[4], (2 * W - 1, HD), jnp.float32) * 0.02}
    _L0_conv_all = _L0_conv_setup()
    _L0_conv_in = {k: v for k, v in _L0_conv_all.items() if k in ('qkv_w', 'qkv_b', 'proj_w', 'proj_b', 'rel_pos_h', 'rel_pos_w')}
    del _L0_conv_all

    def _L0_ffn_setup():
        import jax, jax.numpy as jnp
        import numpy as np
        NUM_EXPERT = 8
        TOP_K = 1
        key = jax.random.key(seed)
        ks = jax.random.split(key, 6)
        B, S, D, E, F = (8, 512, 192, 8, 469)
        scale = 0.02
        return {'x': jax.random.normal(ks[0], (B, S, D), dtype=jnp.float32), 'Wg': jax.random.normal(ks[1], (E, D), dtype=jnp.float32) * scale, 'bg': jnp.zeros((E,), dtype=jnp.float32), 'W1': jax.random.normal(ks[2], (E, F, D), dtype=jnp.float32) * scale, 'W2': jax.random.normal(ks[3], (E, F, D), dtype=jnp.float32) * scale, 'W3': jax.random.normal(ks[4], (E, D, F), dtype=jnp.float32) * scale}
    _L0_ffn_all = _L0_ffn_setup()
    _L0_ffn_in = {k: v for k, v in _L0_ffn_all.items() if k in ('Wg', 'bg', 'W1', 'W2', 'W3')}
    del _L0_ffn_all
    return {'x': x, 'L0_conv_qkv_w': _L0_conv_in['qkv_w'], 'L0_conv_qkv_b': _L0_conv_in['qkv_b'], 'L0_conv_proj_w': _L0_conv_in['proj_w'], 'L0_conv_proj_b': _L0_conv_in['proj_b'], 'L0_conv_rel_pos_h': _L0_conv_in['rel_pos_h'], 'L0_conv_rel_pos_w': _L0_conv_in['rel_pos_w'], 'L0_ffn_Wg': _L0_ffn_in['Wg'], 'L0_ffn_bg': _L0_ffn_in['bg'], 'L0_ffn_W1': _L0_ffn_in['W1'], 'L0_ffn_W2': _L0_ffn_in['W2'], 'L0_ffn_W3': _L0_ffn_in['W3']}

def reference(x, L0_conv_qkv_w, L0_conv_qkv_b, L0_conv_proj_w, L0_conv_proj_b, L0_conv_rel_pos_h, L0_conv_rel_pos_w, L0_ffn_Wg, L0_ffn_bg, L0_ffn_W1, L0_ffn_W2, L0_ffn_W3):
    import jax
    import jax.numpy as jnp

    def _L0_conv_ref(x, qkv_w, qkv_b, proj_w, proj_b, rel_pos_h, rel_pos_w):
        import jax, jax.numpy as jnp
        import numpy as np
        B, H, W, DIM, HEADS = (4, 32, 32, 192, 12)
        HD = DIM // HEADS
        b, h, w, dim = x.shape
        heads = HEADS
        hd = dim // heads
        n = h * w
        scale = hd ** (-0.5)
        xf = x.reshape(b, n, dim)
        qkv = xf @ qkv_w.T + qkv_b
        qkv = qkv.reshape(b, n, 3, heads, hd)
        qkv = jnp.transpose(qkv, (2, 0, 3, 1, 4)).reshape(3, b * heads, n, hd)
        q, k, v = (qkv[0], qkv[1], qkv[2])
        idx_h = jnp.arange(h)[:, None] - jnp.arange(h)[None, :] + (h - 1)
        idx_w = jnp.arange(w)[:, None] - jnp.arange(w)[None, :] + (w - 1)
        Rh = rel_pos_h[idx_h]
        Rw = rel_pos_w[idx_w]
        r_q = q.reshape(b * heads, h, w, hd)
        rel_h = jnp.einsum('bhwc,hkc->bhwk', r_q, Rh)
        rel_w = jnp.einsum('bhwc,wkc->bhwk', r_q, Rw)
        bias = (rel_h[:, :, :, :, None] + rel_w[:, :, :, None, :]).reshape(b * heads, n, n)
        attn = jax.nn.softmax(jnp.einsum('bnd,bmd->bnm', q * scale, k) + bias, axis=-1)
        out = jnp.einsum('bnm,bmd->bnd', attn, v)
        out = out.reshape(b, heads, n, hd).transpose(0, 2, 1, 3).reshape(b, n, dim)
        out = out @ proj_w.T + proj_b
        return out.reshape(b, h, w, dim)

    def _L0_ffn_ref(x, Wg, bg, W1, W2, W3):
        import jax, jax.numpy as jnp
        import numpy as np
        NUM_EXPERT = 8
        TOP_K = 1
        B, S, D = x.shape
        E = Wg.shape[0]
        xf = x.reshape(B * S, D)
        gate = xf @ Wg.T + bg
        vals, idx = jax.lax.top_k(gate, TOP_K)
        probs = jax.nn.softmax(vals, axis=-1)
        dispatch = jnp.sum(jax.nn.one_hot(idx, E, dtype=x.dtype) * probs[..., None], axis=1)
        h = jax.nn.silu(jnp.einsum('td,efd->tef', xf, W1)) * jnp.einsum('td,efd->tef', xf, W2)
        out = jnp.einsum('tef,edf,te->td', h, W3, dispatch)
        return out.reshape(B, S, D)

    def _gn(v, G=32, eps=1e-05):
        B_, H_, W_, C_ = v.shape
        g = v.reshape(B_, H_, W_, G, C_ // G)
        m = jnp.mean(g, axis=(1, 2, 4), keepdims=True)
        s = jnp.var(g, axis=(1, 2, 4), keepdims=True)
        return ((g - m) / jnp.sqrt(s + eps)).reshape(v.shape)

    def _ln_c(v, eps=1e-06):
        m = jnp.mean(v, axis=-1, keepdims=True)
        s = jnp.var(v, axis=-1, keepdims=True)
        return (v - m) / jnp.sqrt(s + eps)

    def _ln_t(v, eps=1e-05):
        m = jnp.mean(v, axis=-1, keepdims=True)
        s = jnp.var(v, axis=-1, keepdims=True)
        return (v - m) / jnp.sqrt(s + eps)

    def _to_tokens(v):
        B_, H_, W_, C_ = v.shape
        return v.reshape(B_, H_ * W_, C_)

    def _from_tokens(t, like):
        return t.reshape(like.shape)
    x = x + _L0_conv_ref(_ln_c(x), L0_conv_qkv_w, L0_conv_qkv_b, L0_conv_proj_w, L0_conv_proj_b, L0_conv_rel_pos_h, L0_conv_rel_pos_w)
    t = _to_tokens(x)
    t = t + _L0_ffn_ref(_ln_t(t), L0_ffn_Wg, L0_ffn_bg, L0_ffn_W1, L0_ffn_W2, L0_ffn_W3)
    x = _from_tokens(t, x)
    return x

_drawn_inputs = setup_inputs


def setup_inputs(seed=0):
    import zlib

    import numpy as np

    out = dict(_drawn_inputs(seed))
    spreads = {'L0_conv_qkv_b': (0.0, 0.326), 'L0_conv_proj_b': (0.0, 0.1), 'L0_ffn_bg': (0.0, 0.79)}
    factors = {'L0_conv_qkv_w': 8.0,
     'L0_conv_rel_pos_h': 8.0,
     'L0_conv_rel_pos_w': 8.0,
     'L0_ffn_Wg': 3.602,
     'L0_ffn_W1': 3.376,
     'L0_ffn_W2': 3.343,
     'L0_ffn_W3': 3.348}
    for name, (base, spread) in spreads.items():
        noise = np.random.default_rng([zlib.crc32(name.encode()), seed]).standard_normal(out[name].shape)
        drawn = base * np.exp(spread * noise) if base else spread * noise
        out[name] = jnp.asarray(drawn.astype(out[name].dtype))
    for name, factor in factors.items():
        out[name] = (out[name] * factor).astype(out[name].dtype)
    return out
```

```python
from contextlib import ExitStack

import concourse.bass as bass
from concourse import mybir

F32 = mybir.dt.float32
F16 = mybir.dt.float16
I32 = mybir.dt.int32
U32 = mybir.dt.uint32
ALU = mybir.AluOpType
ACT = mybir.ActivationFunctionType
AX = mybir.AxisListType.X

P = 128
B, H, W, D = 4, 32, 32, 192
HEADS, HD = 12, 16
N = H * W
T = B * N
TT = T // P
C = D // 2
BH = B * HEADS
HALF = 512
STEPS = T // HALF
TPS = HALF // P
HS = H // 2
KT = N // P
VW = HD + 1
SCALE = HD ** -0.5
EPS_ATT, EPS_FFN = 1e-6, 1e-5


class Shared:
    pass


class Step:

    def __init__(self, n, group, slot, total, known):
        self.n, self.group, self.slot, self.total, self.known = n, group, slot, total, known

    def before(self, k):
        return not self.known or self.n >= k

    def after(self, k):
        return not self.known or self.n + k < self.total


def steps(engine, total, unroll, body):
    groups = total // unroll
    for j in range(unroll):
        body(Step(j, 0, j, total, True))
    if groups > 2:
        with engine.Fori(1, groups - 1) as g:
            for j in range(unroll):
                body(Step(unroll * g + j, g, j, total, False))
    for n in range(max(unroll, unroll * (groups - 1)), total):
        body(Step(n, n // unroll, n % unroll, total, True))


def by_key(half):
    return half.rearrange("p (r i w) -> p i r w", i=2, w=HS)


def as_keys(half):
    return half.rearrange("p (i r w) -> p i r w", i=2, w=HS)


def project(nc, g):
    with ExitStack() as ctx:
        sb = lambda name, shape, dt=F32: ctx.enter_context(nc.sbuf_tensor(name, shape, dt))
        sem = lambda name: ctx.enter_context(nc.semaphore(name))
        w = [sb("qkv_w_top", [C, 3 * D]), sb("qkv_w_bottom", [C + 1, 3 * D])]
        stats = sb("stats", [P, TT, 6])
        mean = sb("mean", [P, TT])
        var, rstd, tmp = sb("var", [P, TT]), sb("rstd", [P, TT]), sb("tmp", [P, TT])
        xn = sb("xn", [P, 2, TPS, D])
        xt = [sb("xt_top", [C, 2, HALF]), sb("xt_bottom", [C + 1, 2, HALF])]
        hi = sb("qk_hi", [C, 2, 4, HALF], F16)
        lo = sb("qk_lo", [C, 2, 4, HALF], F16)
        empty = sb("empty_row_sb", [P, ROW])
        psum = lambda name, shape: ctx.enter_context(nc.psum_tensor(name, shape, F32))
        t_ps = [psum(f"xt_ps{c}", [C, HALF]) for c in range(2)]
        qk_ps = [psum(f"qk_ps{m}", [C, HALF]) for m in range(4)]
        v_ps = [psum(f"v_ps{i}", [P, HALF]) for i in range(2)]

        x_loaded = [sem(f"x_loaded{c}") for c in range(4)]
        consts_loaded = sem("consts_loaded")
        stats_done, chain, root, root_done = sem("stats_done"), sem("att_chain"), sem("att_root"), sem("att_root_done")
        wk_scaled, ones_set = sem("wk_scaled"), sem("ones_set")
        empty_ready, empty_numbered, emptied = sem("empty_ready"), sem("empty_numbered"), sem("emptied")
        xn_ready, xt_ps_ready, xt_ready = sem("xn_ready"), sem("xt_ps_ready"), sem("xt_ready")
        qk_ready = sem("qk_ready")
        hi_done, lo_done = sem("hi_done"), sem("lo_done")
        v_ready, v_copied = sem("v_ready"), sem("v_copied")
        hi_stored = [sem(f"hi_stored{j}") for j in range(2)]
        lo_stored = [sem(f"lo_stored{j}") for j in range(2)]

        block = ctx.enter_context(nc.Block())
        XC = TT // 4

        @block.sync
        def _(sp):
            sp.dma_start(g.x_sb[:, 0:XC, :], g.x_tiles[:, 0:XC, :]).then_inc(x_loaded[0], 16)
            sp.dma_start(w[0][:], g.qkv_wt[0:C, :]).then_inc(consts_loaded, 16)
            sp.dma_start(w[1][0:C, :], g.qkv_wt[C:D, :]).then_inc(consts_loaded, 16)
            sp.dma_start(w[1][C:C + 1, :], g.qkv_b).then_inc(consts_loaded, 16)
            sp.dma_start(g.ident[:], g.ident_dram).then_inc(consts_loaded, 16)
            for c in range(1, 4):
                sp.dma_start(g.x_sb[:, c * XC:(c + 1) * XC, :], g.x_tiles[:, c * XC:(c + 1) * XC, :]).then_inc(x_loaded[c], 16)

            def store(s):
                for part, (src, done, stored) in enumerate(((hi, hi_done, hi_stored), (lo, lo_done, lo_stored))):
                    sp.wait_ge(done, 4 * s.n + 4)
                    for m in range(4):
                        dst = g.qk_split[m // 2, part, bass.ds(s.group * D + m % 2 * C, C), s.slot * HALF:(s.slot + 1) * HALF]
                        sp.dma_start(dst, src[:, s.slot, m, :]).then_inc(stored[s.slot], 16)

            steps(sp, STEPS, 2, store)
            for j in range(2):
                sp.wait_ge(hi_stored[j], 64 * (STEPS // 2))
                sp.wait_ge(lo_stored[j], 64 * (STEPS // 2))

        @block.gpsimd
        def _(pool):
            nc.gpsimd.memset(xt[1][C:C + 1, :, :], 1.0).then_inc(ones_set, 1)
            pool.wait_ge(ones_set, 1)
            nc.gpsimd.memset(g.v_sb[:], 1.0).then_inc(ones_set, 1)
            pool.wait_ge(ones_set, 2)
            nc.gpsimd.memset(empty[:], 0.0).then_inc(empty_ready, 1)
            pool.wait_ge(empty_ready, 1)
            pool.dma_start(empty[:, 2 * D:ROW].bitcast(U32), g.empty_row_dram).then_inc(empty_numbered, 16)
            pool.wait_ge(empty_numbered, 16)
            for i in range(SLOTS_ALL // P):
                pool.dma_start(g.slots_dram[i * P:(i + 1) * P, :], empty[:]).then_inc(emptied, 16)
            pool.wait_ge(emptied, 16 * (SLOTS_ALL // P))

        @block.vector
        def _(dve):
            for c in range(4):
                dve.wait_ge(x_loaded[c], 16)
                with dve.Fori(c * XC, (c + 1) * XC) as t:
                    nc.vector.bn_stats(stats[:, t, :], g.x_sb[:, t, :]).then_inc(stats_done, 1)
            dve.wait_ge(stats_done, TT)
            dve.wait_ge(consts_loaded, 64)
            for half in w:
                nc.vector.tensor_scalar(half[:, D:2 * D], half[:, D:2 * D], SCALE, None, ALU.mult).then_inc(wk_scaled, 1)
            inverse_root(nc, dve, stats, mean, var, rstd, tmp, EPS_ATT, chain, root, root_done)

            def normalize(n, slot, reused):
                if reused:
                    dve.wait_ge(xt_ps_ready, 2 * n - 2)
                for i in range(TPS):
                    t = n * TPS + i
                    nc.vector.tensor_scalar(xn[:, slot, i, :], g.x_sb[:, t, :], mean[:, bass.ds(t, 1)], rstd[:, bass.ds(t, 1)],
                                            ALU.subtract, ALU.mult).then_inc(xn_ready, 1)

            normalize(0, 0, False)

            def step(s):
                if s.after(1):
                    normalize(s.n + 1, 1 - s.slot, s.before(1))
                if s.before(2):
                    dve.wait_ge(lo_stored[s.slot], 64 * s.group)
                for m in range(4):
                    dve.wait_ge(hi_done, 4 * s.n + m + 1)
                    nc.vector.tensor_tensor(lo[:, s.slot, m, :], qk_ps[m][:], hi[:, s.slot, m, :], ALU.subtract).then_inc(lo_done, 1)

            steps(dve, STEPS, 2, step)

        @block.scalar
        def _(act):
            act.wait_ge(root, 1)
            nc.scalar.activation(rstd[:], var[:], ACT.Sqrt).then_inc(root_done, 1)

            def step(s):
                for c in range(2):
                    act.wait_ge(xt_ps_ready, 2 * s.n + c + 1)
                    if s.before(2):
                        act.wait_ge(v_ready, 2 * s.n - 2)
                    nc.scalar.activation(as_keys(xt[c][0:C, s.slot, :]), by_key(t_ps[c][:]), ACT.Copy).then_inc(xt_ready, 1)
                if s.before(2):
                    act.wait_ge(hi_stored[s.slot], 64 * s.group)
                    act.wait_ge(lo_done, 4 * s.n - 4)
                for m in range(4):
                    act.wait_ge(qk_ready, 4 * s.n + m + 1)
                    nc.scalar.activation(hi[:, s.slot, m, :], qk_ps[m][:], ACT.Copy).then_inc(hi_done, 1)
                if s.n == 0 if s.known else False:
                    act.wait_ge(ones_set, 2)
                for i in range(2):
                    act.wait_ge(v_ready, 2 * s.n + i + 1)
                    tiles = g.v_sb[:, bass.ds(s.group * HEADS, HEADS), s.slot * 4 + 2 * i:s.slot * 4 + 2 * i + 2, 0:HD]
                    nc.scalar.activation(tiles.rearrange("p h t d -> p t h d"),
                                         v_ps[i][:, 0:2 * D].rearrange("p (t h d) -> p t h d", t=2, h=HEADS),
                                         ACT.Copy).then_inc(v_copied, 1)

            steps(act, STEPS, 2, step)

        @block.tensor
        def _(pe):
            pe.wait_ge(consts_loaded, 64)
            pe.wait_ge(wk_scaled, 2)
            pe.wait_ge(ones_set, 2)

            def step(s):
                pe.wait_ge(xn_ready, TPS * s.n + TPS)
                for c in range(2):
                    if s.before(1):
                        pe.wait_ge(xt_ready, 2 * s.n)
                    for i in range(TPS):
                        last = nc.tensor.transpose(t_ps[c][:, i * P:(i + 1) * P], xn[:, s.slot, i, c * C:(c + 1) * C], g.ident[:])
                    last.then_inc(xt_ps_ready, 1)
                pe.wait_ge(xt_ready, 2 * s.n + 2)
                for m in range(4):
                    if s.before(1):
                        pe.wait_ge(lo_done, 4 * s.n + m - 3)
                    for c in range(2):
                        tokens = xt[c][:, s.slot, :]
                        if m < 2:
                            tokens = tokens.rearrange("p (i r w) -> p r i w", i=2, w=HS)
                        last = nc.tensor.matmul(qk_ps[m][:], w[c][:, m * C:(m + 1) * C], tokens,
                                                start=(c == 0), stop=(c == 1))
                    last.then_inc(qk_ready, 1)
                for i in range(2):
                    if s.before(1):
                        pe.wait_ge(v_copied, 2 * s.n + i - 1)
                    for t in range(2):
                        for c in range(2):
                            keys = xt[c][:, s.slot, (2 * i + t) * P:(2 * i + t + 1) * P]
                            last = nc.tensor.matmul(v_ps[i][:, t * D:(t + 1) * D], keys, w[c][:, 2 * D:3 * D],
                                                    start=(c == 0), stop=(c == 1))
                    last.then_inc(v_ready, 1)

            steps(pe, STEPS, 2, step)


def relative_positions(nc, g):
    Q_ROWS = 4 * HD
    R = 2 * H - 1
    PAIRS = HEADS // 2
    with ExitStack() as ctx:
        sb = lambda name, shape, dt=F32: ctx.enter_context(nc.sbuf_tensor(name, shape, dt))
        sem = lambda name: ctx.enter_context(nc.semaphore(name))
        table = sb("table", [Q_ROWS, 2 * R])
        low_rows = sb("low_rows", [Q_ROWS, 1])
        table_hi = sb("table_hi", [Q_ROWS, 2 * R], F16)
        table_masked = sb("table_masked", [Q_ROWS, 2 * R])
        table_parts = sb("table_parts", [Q_ROWS, 2 * R], F16)
        q = sb("q_stack", [Q_ROWS, 2, 2, B, N], F16)
        hi = sb("rel_hi", [P, 2, 2, N], F16)
        lo = sb("rel_lo", [P, 2, 2, N], F16)
        rel_ps = [ctx.enter_context(nc.psum_tensor(f"rel_ps{axis}", [P, 2 * N], F32)) for axis in range(2)]

        table_loaded, table_split = sem("table_loaded"), sem("table_split")
        q_loaded = [sem(f"q_loaded{j}") for j in range(2)]
        rel_ready, hi_done, lo_done = sem("rel_ready"), sem("rel_hi_done"), sem("rel_lo_done")
        hi_stored = [sem(f"rel_hi_stored{axis}") for axis in range(2)]
        lo_stored = [sem(f"rel_lo_stored{axis}") for axis in range(2)]
        block = ctx.enter_context(nc.Block())

        @block.gpsimd
        def _(pool):
            for r in range(4):
                for axis in range(2):
                    pool.dma_start(table[r * HD:(r + 1) * HD, axis * R:(axis + 1) * R], g.rel_tables[axis]).then_inc(table_loaded, 16)
            pool.dma_start(low_rows[:], g.low_rows_dram).then_inc(table_loaded, 16)

            def load(s):
                if s.before(2):
                    pool.wait_ge(rel_ready, 2 * s.n - 2)
                for h in range(2):
                    for r in range(4):
                        src = g.qk_heads[0, r // 2, 2 * s.n + h]
                        pool.dma_start(q[r * HD:(r + 1) * HD, s.slot, h, :, :], src).then_inc(q_loaded[s.slot], 16)

            steps(pool, PAIRS, 2, load)

        @block.sync
        def _(sp):
            def store(s):
                for axis in range(2):
                    for part, (src, done, stored) in enumerate(((hi, hi_done, hi_stored), (lo, lo_done, lo_stored))):
                        sp.wait_ge(done, 2 * s.n + axis + 1)
                        for b in range(B):
                            sp.dma_start(g.rel_split[axis, part, b, bass.ds(2 * s.n, 2)].rearrange("h r n -> r h n"),
                                         src[b * H:(b + 1) * H, axis, :, :]).then_inc(stored[axis], 16)

            steps(sp, PAIRS, 2, store)
            for axis in range(2):
                sp.wait_ge(hi_stored[axis], 64 * PAIRS)
                sp.wait_ge(lo_stored[axis], 64 * PAIRS)

        @block.tensor
        def _(pe):
            pe.wait_ge(table_split, 3)

            def products(s):
                pe.wait_ge(q_loaded[s.slot], 128 * s.group + 128)
                for axis in range(2):
                    if s.before(1):
                        pe.wait_ge(lo_done, 2 * s.n + axis - 1)
                    for i in range(H):
                        rows = table_parts[:, axis * R + H - 1 - i:axis * R + 2 * H - 1 - i]
                        for b in range(B):
                            image = q[:, s.slot, :, b, :].rearrange("p h (r w) -> p h r w", w=W)
                            last = nc.tensor.matmul(rel_ps[axis][b * H:(b + 1) * H, i * 2 * W:(i + 1) * 2 * W], rows,
                                                    image[:, :, i, :] if axis == 0 else image[:, :, :, i], start=True, stop=True)
                    last.then_inc(rel_ready, 1)

            steps(pe, PAIRS, 2, products)

        def product(axis, h):
            return rel_ps[axis][:].rearrange("p (i h j) -> p h i j", h=2, j=W)[:, h]

        def by_query(part, axis, h):
            return part[:, axis, h, :].rearrange("p (r w) -> p r w" if axis == 0 else "p (r w) -> p w r", w=W)

        @block.scalar
        def _(act):
            act.wait_ge(table_loaded, 16 * 9)
            nc.scalar.activation(table_hi[:], table[:], ACT.Copy).then_inc(table_split, 1)

            def high_parts(s):
                for axis in range(2):
                    act.wait_ge(rel_ready, 2 * s.n + axis + 1)
                    if s.before(1):
                        act.wait_ge(hi_stored[axis], 64 * s.n)
                        act.wait_ge(lo_done, 2 * s.n + axis - 1)
                    for h in range(2):
                        last = nc.scalar.activation(by_query(hi, axis, h), product(axis, h), ACT.Copy)
                    last.then_inc(hi_done, 1)

            steps(act, PAIRS, 2, high_parts)

        @block.vector
        def _(dve):
            dve.wait_ge(table_split, 1)
            nc.vector.tensor_scalar(table_masked[:], table_hi[:], low_rows[:], None, ALU.mult).then_inc(table_split, 1)
            dve.wait_ge(table_split, 2)
            nc.vector.tensor_tensor(table_parts[:], table[:], table_masked[:], ALU.subtract).then_inc(table_split, 1)

            def low_parts(s):
                for axis in range(2):
                    dve.wait_ge(hi_done, 2 * s.n + axis + 1)
                    if s.before(1):
                        dve.wait_ge(lo_stored[axis], 64 * s.n)
                    for h in range(2):
                        last = nc.vector.tensor_tensor(by_query(lo, axis, h), product(axis, h), by_query(hi, axis, h), ALU.subtract)
                    last.then_inc(lo_done, 1)

            steps(dve, PAIRS, 2, low_parts)


def attention(nc, g):
    QK_ROWS = 3 * HD
    REL_ROW = QK_ROWS
    MAX_ROW = QK_ROWS + 4 * HS
    ROWS = MAX_ROW + 1
    SLOTS = 4
    QUARTERS = 4
    PAIR_TILES = KT // 2
    GROUP = 4
    RING = 2 * GROUP
    LOADS = 14
    with ExitStack() as ctx:
        sb = lambda name, shape, dt=F32: ctx.enter_context(nc.sbuf_tensor(name, shape, dt))
        sem = lambda name: ctx.enter_context(nc.semaphore(name))
        q_side = [sb(f"q_side{j}", [ROWS, QUARTERS, N], F16) for j in range(SLOTS)]
        k_side = [sb(f"k_side{j}", [ROWS, N], F16) for j in range(SLOTS)]
        values = [sb(f"values{j}", [P, KT, 2 * HD]) for j in range(SLOTS)]
        probs = sb("probs", [P, RING, HALF])
        neg_max = sb("neg_max", [P, 2, KT], F16)
        max_rows = sb("max_rows", [KT, 2, P], F16)
        ident16 = sb("ident16", [P, P], F16)
        out_t = sb("out_t", [P, HALF])
        fold = sb("fold", [P, 4 * HD])
        recip = sb("recip", [P, KT])
        max_ps = [ctx.enter_context(nc.psum_tensor(f"max_ps{i}", [P, N], F32)) for i in range(2)]
        ring_ps = [ctx.enter_context(nc.psum_tensor(f"ring_ps{i}", [P, HALF], F32)) for i in range(3)]
        out_ps = ctx.enter_context(nc.psum_tensor("out_ps", [P, HALF], F32))
        MAX_AT, FOLD_AT, TURN = 8, 13, 18
        FOLDED = 4 * 4 * HD
        folded_sb = sb("folded", [P, FOLDED])

        def score_at(k):
            return k + (k >= 8) + (k >= 12)

        consts_loaded, zeroed = sem("att_consts_loaded"), sem("values_zeroed")
        ident_cast = sem("ident_cast")
        loaded = [sem(f"loaded{j}") for j in range(SLOTS)]
        max_loaded = [sem(f"max_loaded{j}") for j in range(SLOTS)]
        values_ready = sem("values_ready")
        raw_ready, tile_max = sem("raw_ready"), sem("tile_max")
        max_t_ready, max_copied = sem("max_t_ready"), sem("max_copied")
        scores_ready, exp_done, group_done = sem("scores_ready"), sem("exp_done"), sem("group_done")
        out_copied, folded, fold_copied = sem("out_copied"), sem("fold_ready"), sem("fold_copied")
        recip_done, att_done = sem("recip_done"), sem("att_done")
        block = ctx.enter_context(nc.Block())

        @block.sync
        def _(sp):
            for j in range(SLOTS):
                sp.dma_start(k_side[j][REL_ROW:ROWS, :], g.key_rows_dram).then_inc(consts_loaded, 16)
            sp.dma_start(fold[:], g.fold_dram).then_inc(consts_loaded, 16)

            def load(n, slot):
                both = lambda ap: ap.rearrange("r (o n) -> r o n", o=1).broadcast_to([ap.shape[0], QUARTERS, N])
                inc = loaded[slot]
                q_hi, q_lo, k_hi, k_lo = (g.qk_split[i, part, bass.ds(n * HD, HD), :] for i in range(2) for part in range(2))
                q = q_side[slot]
                for at, src in ((0, q_hi), (HD, q_hi), (2 * HD, q_lo)):
                    sp.dma_start(q[at:at + HD, :, :], both(src)).then_inc(inc, 16)
                for at, src in ((0, k_hi), (HD, k_lo), (2 * HD, k_hi)):
                    sp.dma_start(k_side[slot][at:at + HD, :], src).then_inc(inc, 16)

            def load_rel(n, slot):
                inc = loaded[slot]
                q = q_side[slot]
                for part in range(2):
                    for axis in range(2):
                        at = REL_ROW + (2 * part + axis) * HS
                        halves = g.rel_pairs[axis, part, n].rearrange("(a r) n -> r a n", a=2)
                        dst = q[at:at + HS, :, :].rearrange("p (i j) n -> p i j n", i=2)
                        for other in range(2):
                            where = dst[:, :, other, :] if axis == 0 else dst[:, other, :, :]
                            sp.dma_start(where, halves).then_inc(inc, 16)

            def fill(n, slot):
                load(n, slot)
                load_rel(n, slot)

            for n in range(SLOTS - 1):
                fill(n, n)

            def store_max(n, slot):
                sp.wait_ge(max_copied, n + 1)
                for quarter in range(QUARTERS):
                    sp.dma_start(q_side[slot][MAX_ROW:ROWS, quarter, :].rearrange("o (t p) -> o t p", p=P),
                                 max_rows[:, slot % 2, :]).then_inc(max_loaded[slot], 16)

            store_max(0, 0)

            def step(s):
                if s.after(3):
                    if s.before(1):
                        sp.wait_ge(scores_ready, 16 * s.n)
                    fill(s.n + 3, (s.slot + 3) % SLOTS)
                if s.after(1):
                    store_max(s.n + 1, (s.slot + 1) % SLOTS)

            steps(sp, BH, SLOTS, step)

        @block.gpsimd
        def _(pool):
            for j in range(SLOTS):
                nc.gpsimd.memset(values[j][:], 0.0).then_inc(zeroed, 1)
            pool.wait_ge(zeroed, SLOTS)

            def step(s):
                if s.before(4):
                    pool.wait_ge(group_done, PAIR_TILES * (s.n - SLOTS + 1))
                nc.gpsimd.tensor_copy(values[s.slot][:, :, 0:VW], g.v_sb[:, s.n]).then_inc(values_ready, 1)

            steps(pool, BH, SLOTS, step)

        @block.tensor
        def _(pe):
            pe.wait_ge(consts_loaded, 16 * (SLOTS + 1))
            pe.wait_ge(ident_cast, 1)

            def raw_scores(n, slot, t, reused):
                if reused:
                    pe.wait_ge(tile_max, KT * n + t - 1)
                for quarter in range(QUARTERS):
                    keys = slice(quarter * 2 * P, (quarter + 1) * 2 * P)
                    last = nc.tensor.matmul(max_ps[t % 2][:, keys], q_side[slot][0:MAX_ROW, quarter, t * P:(t + 1) * P],
                                            k_side[slot][0:MAX_ROW, keys], start=True, stop=True, skip_group_check=True)
                last.then_inc(raw_ready, 1)

            def bank_free(s, at):
                at -= 3
                back = 0
                while True:
                    if at < 0:
                        at, back = at + TURN, 1
                        if not s.before(1):
                            return
                    if at == MAX_AT and (back or s.after(1)):
                        return pe.wait_ge(max_copied, s.n - back + 2)
                    if at == FOLD_AT and (s.before(1) if not back else s.before(2)):
                        return pe.wait_ge(fold_copied, s.n - back)
                    if at not in (MAX_AT, FOLD_AT):
                        k = at - (at > MAX_AT) - (at > FOLD_AT)
                        return pe.wait_ge(exp_done, KT * 2 * (s.n - back) + k + 1)
                    at -= 3

            def transpose_max(n, slot):
                pe.wait_ge(tile_max, KT * (n + 1))
                nc.tensor.matmul(ring_ps[MAX_AT % 3][0:KT, 0:P], neg_max[:, slot % 2, :], ident16[:],
                                 start=True, stop=True).then_inc(max_t_ready, 1)

            def scores(s, u, i):
                tile, at = 2 * u + i // 2, score_at(GROUP * u + i)
                bank_free(s, at)
                nc.tensor.matmul(ring_ps[at % 3][:], k_side[s.slot][:, tile * P:(tile + 1) * P],
                                 q_side[s.slot][:, tile // 2, (i % 2) * HALF:(i % 2 + 1) * HALF],
                                 start=True, stop=True).then_inc(scores_ready, 1)

            def weighted_values(n, slot, u):
                pe.wait_ge(exp_done, 16 * n + GROUP * u + GROUP)
                for i in range(GROUP):
                    tile = 2 * u + i // 2
                    last = nc.tensor.matmul(out_ps[i * 2 * HD:(i + 1) * 2 * HD, :], values[slot][:, tile, :],
                                            probs[:, u % 2 * GROUP + i, :], start=(u == 0), stop=(u == PAIR_TILES - 1),
                                            tile_position=(0, i * 2 * HD))
                last.then_inc(group_done, 1)

            def fold_out(n):
                pe.wait_ge(out_copied, n + 1)
                for blk in range(4):
                    last = nc.tensor.matmul(ring_ps[FOLD_AT % 3][:, blk * 4 * HD:(blk + 1) * 4 * HD], out_t[:, blk * P:(blk + 1) * P],
                                            fold[:], start=True, stop=True, skip_group_check=True)
                last.then_inc(folded, 1)

            for n, tiles in ((0, KT), (1, 6)):
                pe.wait_ge(loaded[n], 16 * LOADS)
                for t in range(tiles):
                    raw_scores(n, n, t, KT * n + t >= 2)
                if n == 0:
                    transpose_max(0, 0)

            def step(s):
                j = s.slot
                one, two, back = (j + 1) % SLOTS, (j + 2) % SLOTS, (j - 1) % SLOTS
                for u in range(PAIR_TILES):
                    if u == 0:
                        pe.wait_ge(max_loaded[j], 64 * (s.group + 1))
                    if u == 1 and s.after(2):
                        pe.wait_ge(loaded[two], 16 * LOADS * (s.group + (2 if j >= 2 else 1)))
                    for i in range(GROUP):
                        scores(s, u, i)
                        if i in (1, 2):
                            if u == 0 and s.after(1):
                                raw_scores(s.n + 1, one, 6 + i - 1, True)
                            if u >= 1 and s.after(2):
                                raw_scores(s.n + 2, two, 2 * (u - 1) + i - 1, True)
                    if u == 0 and s.before(1):
                        weighted_values(s.n - 1, back, PAIR_TILES - 1)
                    if u == 1:
                        pe.wait_ge(values_ready, s.n + 1)
                        if s.before(1):
                            pe.wait_ge(out_copied, s.n)
                    if u >= 1:
                        weighted_values(s.n, j, u - 1)
                    if u == 1 and s.after(1):
                        bank_free(s, MAX_AT)
                        transpose_max(s.n + 1, one)
                    if u == 2 and s.before(1):
                        bank_free(s, FOLD_AT)
                        fold_out(s.n - 1)

            steps(pe, BH, SLOTS, step)
            weighted_values(BH - 1, (BH - 1) % SLOTS, PAIR_TILES - 1)
            pe.wait_ge(exp_done, 2 * KT * BH)
            fold_out(BH - 1)

        @block.scalar
        def _(act):
            nc.scalar.activation(ident16[:], g.ident[:], ACT.Copy).then_inc(ident_cast, 1)

            def copy_max(n, slot, fills):
                act.wait_ge(max_t_ready, n + 1)
                if fills is not None:
                    act.wait_ge(max_loaded[(slot - 2) % SLOTS], 64 * fills)
                nc.scalar.activation(max_rows[:, slot % 2, :], ring_ps[MAX_AT % 3][0:KT, 0:P], ACT.Copy).then_inc(max_copied, 1)

            def copy_out(n, reused):
                act.wait_ge(group_done, PAIR_TILES * (n + 1))
                if reused:
                    act.wait_ge(folded, n)
                nc.scalar.activation(out_t[:], out_ps[:], ACT.Copy).then_inc(out_copied, 1)

            def copy_fold(n, reused):
                act.wait_ge(folded, n + 1)
                if reused:
                    act.wait_ge(att_done, n)
                nc.scalar.activation(folded_sb[:], ring_ps[FOLD_AT % 3][:, 0:FOLDED], ACT.Copy).then_inc(fold_copied, 1)

            copy_max(0, 0, None)

            def step(s):
                for u in range(PAIR_TILES):
                    for i in range(GROUP):
                        if u == 1 and i == 2 and s.before(1):
                            copy_out(s.n - 1, s.before(2))
                        if i == 0 and (s.before(1) or u >= 2):
                            act.wait_ge(group_done, PAIR_TILES * s.n + u - 1)
                        act.wait_ge(scores_ready, 16 * s.n + GROUP * u + i + 1)
                        nc.scalar.activation(probs[:, u % 2 * GROUP + i, :], ring_ps[score_at(GROUP * u + i) % 3][:], ACT.Exp).then_inc(exp_done, 1)
                    if u == 1 and s.after(1):
                        one = (s.slot + 1) % SLOTS
                        earlier = None if not s.before(1) else (s.group + 1 if s.slot >= 1 else s.group)
                        copy_max(s.n + 1, one, earlier)
                    if u == 2 and s.before(1):
                        copy_fold(s.n - 1, s.before(2))

            steps(act, BH, SLOTS, step)
            copy_out(BH - 1, True)
            copy_fold(BH - 1, True)

        @block.vector
        def _(dve):
            def take_max(n, slot, t, reused):
                dve.wait_ge(raw_ready, KT * n + t + 1)
                if reused:
                    dve.wait_ge(max_t_ready, n - 1)
                nc.vector.tensor_reduce(neg_max[:, slot % 2, t:t + 1], max_ps[t % 2][:], AX, ALU.max, negate=True).then_inc(tile_max, 1)

            def normalize(n, reused):
                dve.wait_ge(fold_copied, n + 1)
                by_block = folded_sb[:].rearrange("p (b h c) -> p b h c", b=4, h=2)
                if reused:
                    dve.wait_ge(att_done, n)
                nc.vector.reciprocal(recip[:].rearrange("p (h b) -> p b h", h=2), by_block[:, :, :, HD]).then_inc(recip_done, 1)
                dve.wait_ge(recip_done, n + 1)
                dst = g.att_sb[:, n].rearrange("p (h b) d -> p b h d", h=2)
                by = recip[:].rearrange("p (h b o) -> p b h o", h=2, o=1).broadcast_to([P, 4, 2, HD])
                nc.vector.tensor_tensor(dst, by_block[:, :, :, 0:HD], by, ALU.mult).then_inc(att_done, 1)

            for n, tiles in ((0, KT), (1, 6)):
                for t in range(tiles):
                    take_max(n, n, t, False)

            def step(s):
                for u in range(PAIR_TILES):
                    for i in range(2):
                        if u == 0 and s.after(1):
                            take_max(s.n + 1, s.slot + 1, 6 + i, False)
                        if u >= 1 and s.after(2):
                            take_max(s.n + 2, s.slot + 2, 2 * (u - 1) + i, u == 1 and i == 0)
                    if u == 2 and s.before(1):
                        normalize(s.n - 1, s.before(2))

            steps(dve, BH, SLOTS, step)
            normalize(BH - 1, True)


FT = 256
EXPERTS, F = 8, 469
FC = 118
CHUNKS = [(c * FC, min(FC, F - c * FC)) for c in range(-(-F // FC))]
FFN_TILES = T // FT + EXPERTS - 1
SLOTS_ALL = FFN_TILES * FT
ROW = 2 * D + 1


def gate(nc, g):
    with ExitStack() as ctx:
        sb = lambda name, shape, dt=F32: ctx.enter_context(nc.sbuf_tensor(name, shape, dt))
        sem = lambda name: ctx.enter_context(nc.semaphore(name))
        w = [sb("proj_w_top", [C, D]), sb("proj_w_bottom", [C + 1, D])]
        wg = [sb("gate_w_top", [C, EXPERTS]), sb("gate_w_bottom", [C + 1, EXPERTS])]
        att = sb("att", [P, 2, TPS, D])
        at = [sb("at_top", [C, 2, HALF]), sb("at_bottom", [C + 1, 2, HALF])]
        stats = sb("stats2", [P, TT, 6])
        mean = sb("mean2", [P, TT])
        var, rstd, tmp = sb("var2", [P, TT]), sb("rstd2", [P, TT]), sb("tmp2", [P, TT])
        tn = sb("tn", [P, 2, TPS, D])
        psum = lambda name, shape: ctx.enter_context(nc.psum_tensor(name, shape, F32))
        t_ps = [psum(f"at_ps{c}", [C, HALF]) for c in range(2)]
        p_ps = [psum(f"proj_ps{i}", [P, HALF]) for i in range(4)]
        g_ps = [psum(f"gate_ps{i}", [P, TPS * EXPERTS]) for i in range(2)]

        loaded, ones_set, att_ready = sem("gate_loaded"), sem("gate_ones"), sem("att_ready")
        at_ps_ready, at_ready, proj_ready, x1_ready = sem("at_ps_ready"), sem("at_ready"), sem("proj_ready"), sem("x1_ready")
        stats_done, chain = sem("stats2_done"), sem("ffn_chain")
        root, root_done, tn_ready, tn_kept = sem("root"), sem("root_done"), sem("tn_ready"), sem("tn_kept")
        tt_ps_ready, tt_ready, gate_ready, gate_copied = sem("tt_ps_ready"), sem("tt_ready"), sem("gate_ready"), sem("gate_copied")
        block = ctx.enter_context(nc.Block())

        @block.sync
        def _(sp):
            sp.dma_start(w[0][:], g.proj_wt[0:C, :]).then_inc(loaded, 16)
            sp.dma_start(w[1][0:C, :], g.proj_wt[C:D, :]).then_inc(loaded, 16)
            sp.dma_start(w[1][C:C + 1, :], g.proj_b).then_inc(loaded, 16)
            sp.dma_start(wg[0][:], g.gate_wt[0:C, :]).then_inc(loaded, 16)
            sp.dma_start(wg[1][0:C, :], g.gate_wt[C:D, :]).then_inc(loaded, 16)
            sp.dma_start(wg[1][C:C + 1, :], g.gate_b).then_inc(loaded, 16)

        @block.gpsimd
        def _(pool):
            nc.gpsimd.memset(at[1][C:C + 1, :, :], 1.0).then_inc(ones_set, 1)
            pool.wait_ge(ones_set, 1)

            def gather_heads(s):
                if s.before(2):
                    pool.wait_ge(at_ps_ready, 2 * s.n - 2)
                src = g.att_sb[:, bass.ds(s.group * HEADS, HEADS), s.slot * TPS:(s.slot + 1) * TPS, :]
                nc.gpsimd.tensor_copy(att[:, s.slot].rearrange("p t (h d) -> p t h d", h=HEADS),
                                      src.rearrange("p h t d -> p t h d")).then_inc(att_ready, 1)

            steps(pool, STEPS, 2, gather_heads)

            def keep(s):
                pool.wait_ge(tn_ready, TPS * s.n + TPS)
                nc.gpsimd.tensor_copy(g.t_sb[:, bass.ds(TPS * s.n, TPS), :], tn[:, s.slot]).then_inc(tn_kept, 1)

            steps(pool, STEPS, 2, keep)

        @block.tensor
        def _(pe):
            pe.wait_ge(loaded, 96)
            pe.wait_ge(ones_set, 1)

            def transposes(src, slot, ready):
                for c in range(2):
                    for i in range(TPS):
                        last = nc.tensor.transpose(t_ps[c][:, i * P:(i + 1) * P], src[:, slot, i, c * C:(c + 1) * C], g.ident[:])
                    last.then_inc(ready, 1)

            def project_out(s):
                pe.wait_ge(att_ready, s.n + 1)
                if s.before(1):
                    pe.wait_ge(at_ready, 2 * s.n)
                transposes(att, s.slot, at_ps_ready)
                pe.wait_ge(at_ready, 2 * s.n + 2)
                if s.before(2):
                    pe.wait_ge(x1_ready, 2 * s.n - 2)
                for i in range(TPS):
                    for c in range(2):
                        last = nc.tensor.matmul(p_ps[2 * s.slot + i // 2][:, i % 2 * D:(i % 2 + 1) * D],
                                                at[c][:, s.slot, i * P:(i + 1) * P], w[c][:], start=(c == 0), stop=(c == 1))
                    if i % 2:
                        last.then_inc(proj_ready, 1)

            steps(pe, STEPS, 2, project_out)

            def gates(s):
                pe.wait_ge(tn_ready, TPS * s.n + TPS)
                if s.before(1):
                    pe.wait_ge(tt_ready, 2 * s.n)
                transposes(tn, s.slot, tt_ps_ready)
                pe.wait_ge(tt_ready, 2 * s.n + 2)
                if s.before(2):
                    pe.wait_ge(gate_copied, s.n - 1)
                for i in range(TPS):
                    for c in range(2):
                        last = nc.tensor.matmul(g_ps[s.slot][:, i * EXPERTS:(i + 1) * EXPERTS], at[c][:, s.slot, i * P:(i + 1) * P],
                                                wg[c][:], start=(c == 0), stop=(c == 1))
                last.then_inc(gate_ready, 1)

            steps(pe, STEPS, 2, gates)

        @block.scalar
        def _(act):
            def copy_at(s):
                for c in range(2):
                    act.wait_ge(at_ps_ready, 2 * s.n + c + 1)
                    if s.before(2):
                        act.wait_ge(proj_ready, 2 * s.n - 2)
                    nc.scalar.activation(at[c][0:C, s.slot, :], t_ps[c][:], ACT.Copy).then_inc(at_ready, 1)

            steps(act, STEPS, 2, copy_at)
            act.wait_ge(root, 1)
            nc.scalar.activation(rstd[:], var[:], ACT.Sqrt).then_inc(root_done, 1)

            def copy_tt(s):
                for c in range(2):
                    act.wait_ge(tt_ps_ready, 2 * s.n + c + 1)
                    if s.before(2):
                        act.wait_ge(gate_ready, s.n - 1)
                    else:
                        act.wait_ge(proj_ready, 2 * STEPS)
                    nc.scalar.activation(at[c][0:C, s.slot, :], t_ps[c][:], ACT.Copy).then_inc(tt_ready, 1)
                act.wait_ge(gate_ready, s.n + 1)
                nc.scalar.activation(g.gates[:, bass.ds(TPS * s.n, TPS), :], g_ps[s.slot][:], ACT.Copy).then_inc(gate_copied, 1)

            steps(act, STEPS, 2, copy_tt)

        @block.vector
        def _(dve):
            def residual(s):
                for i in range(2):
                    dve.wait_ge(proj_ready, 2 * s.n + i + 1)
                    x = g.x_sb[:, bass.ds(TPS * s.n + 2 * i, 2), :]
                    nc.vector.tensor_tensor(x, p_ps[2 * s.slot + i][:, 0:2 * D].rearrange("p (t d) -> p t d", t=2), x,
                                            ALU.add).then_inc(x1_ready, 1)
                for i in range(TPS):
                    dve.wait_ge(x1_ready, 2 * s.n + i // 2 + 1)
                    t = TPS * s.n + i
                    nc.vector.bn_stats(stats[:, t, :], g.x_sb[:, t, :]).then_inc(stats_done, 1)

            steps(dve, STEPS, 2, residual)
            dve.wait_ge(stats_done, TT)
            inverse_root(nc, dve, stats, mean, var, rstd, tmp, EPS_FFN, chain, root, root_done)

            def normalize(s):
                if s.before(2):
                    dve.wait_ge(tt_ps_ready, 2 * s.n - 2)
                    dve.wait_ge(tn_kept, s.n - 1)
                for i in range(TPS):
                    t = TPS * s.n + i
                    nc.vector.tensor_scalar(tn[:, s.slot, i, :], g.x_sb[:, t, :], mean[:, bass.ds(t, 1)], rstd[:, bass.ds(t, 1)],
                                            ALU.subtract, ALU.mult).then_inc(tn_ready, 1)

            steps(dve, STEPS, 2, normalize)


def inverse_root(nc, dve, stats, mean, var, rstd, tmp, eps, chain, root, root_done):
    done = [0]

    def then(instruction):
        done[0] += 1
        instruction.then_inc(chain, 1)
        dve.wait_ge(chain, done[0])

    tt = nc.vector.tensor_tensor
    then(tt(tmp[:], stats[:, :, 1], stats[:, :, 4], ALU.subtract))
    then(tt(tmp[:], tmp[:], tmp[:], ALU.mult))
    then(tt(mean[:], stats[:, :, 1], stats[:, :, 4], ALU.add))
    then(nc.vector.tensor_scalar(mean[:], mean[:], 0.5, None, ALU.mult))
    then(tt(var[:], stats[:, :, 2], stats[:, :, 5], ALU.add))
    then(nc.vector.tensor_scalar(var[:], var[:], 1.0 / D, eps, ALU.mult, ALU.add))
    then(nc.vector.tensor_scalar(tmp[:], tmp[:], 0.25, None, ALU.mult))
    tt(var[:], var[:], tmp[:], ALU.add).then_inc(root, 1)
    dve.wait_ge(root, 1)
    dve.wait_ge(root_done, 1)
    then(nc.vector.reciprocal(rstd[:], rstd[:]))
    then(tt(tmp[:], rstd[:], rstd[:], ALU.mult))
    then(tt(tmp[:], tmp[:], var[:], ALU.mult))
    then(nc.vector.tensor_scalar(tmp[:], tmp[:], -0.5, 1.5, ALU.mult, ALU.add))
    then(tt(rstd[:], rstd[:], tmp[:], ALU.mult))


def route(nc, g):
    E = EXPERTS
    FULL = T // FT
    with ExitStack() as ctx:
        sb = lambda name, shape, dt=F32: ctx.enter_context(nc.sbuf_tensor(name, shape, dt))
        sem = lambda name: ctx.enter_context(nc.semaphore(name))
        tri, ones = sb("tri", [P, P]), sb("ones", [P, P])
        expert, run, fills, tile_no = (sb("expert", [P, E, TT]), sb("run", [P, E, TT]), sb("fills", [P, E, FULL]), sb("tile_no", [P, FFN_TILES, E]))
        token = sb("token", [P, TT], U32)
        best, which, hot, cand = sb("best", [P, TT]), sb("which", [P, TT]), sb("hot", [P, E, TT]), sb("cand", [P, TT, E])
        total, upto, place = sb("total", [P, E, TT]), sb("upto", [P, E, TT]), sb("place", [P, E, TT])
        over, tiles, ends, before = sb("over", [P, E, FULL]), sb("tiles", [P, E]), sb("ends", [P, E]), sb("before_", [P, E])
        passed, experts_f, slot_f, slot = sb("passed", [P, FFN_TILES, E]), sb("experts_f", [P, FFN_TILES]), sb("slot_f", [P, TT]), sb("slot", [P, TT], U32)
        rows = sb("rows", [P, TT, ROW])
        count_ps = ctx.enter_context(nc.psum_tensor("count_ps", [P, 2 * E * TT], F32))

        loaded, chain, hot_ready, counted = sem("route_loaded"), sem("route_chain"), sem("hot_ready"), sem("counted")
        rows_ready, slot_ready, scattered = sem("rows_ready"), sem("slot_ready"), sem("scattered")
        block = ctx.enter_context(nc.Block())

        @block.sync
        def _(sp):
            for dst, src in ((tri, g.tri_dram), (ones, g.ones_dram), (expert, g.expert_dram), (run, g.run_dram),
                             (fills, g.fills_dram), (tile_no, g.tile_no_dram), (token, g.token_dram)):
                sp.dma_start(dst[:], src).then_inc(loaded, 16)

        @block.tensor
        def _(pe):
            pe.wait_ge(loaded, 16 * 7)
            pe.wait_ge(hot_ready, 1)
            flat = hot[:].rearrange("p e t -> p (e t)")
            nc.tensor.matmul(count_ps[:, 0:E * TT], tri[:], flat, start=True, stop=True, skip_group_check=True)
            nc.tensor.matmul(count_ps[:, E * TT:], ones[:], flat, start=True, stop=True, skip_group_check=True).then_inc(counted, 1)

        @block.scalar
        def _(act):
            act.wait_ge(loaded, 16 * 7)
            nc.scalar.activation(rows[:, :, 0:D], g.t_sb[:], ACT.Copy).then_inc(rows_ready, 1)
            nc.scalar.activation(rows[:, :, D:2 * D], g.x_sb[:], ACT.Copy).then_inc(rows_ready, 1)

        @block.vector
        def _(dve):
            done = [0]

            def then(instruction):
                done[0] += 1
                instruction.then_inc(chain, 1)
                dve.wait_ge(chain, done[0])

            dve.wait_ge(loaded, 16 * 7)
            then(nc.vector.tensor_copy(rows[:, :, 2 * D:ROW].bitcast(U32), token[:].rearrange("p (t o) -> p t o", o=1)))
            by_token = lambda table: table[:].rearrange("p e t -> p t e")
            wide = lambda ap, n: ap.rearrange("p (t o) -> p t o", o=1).broadcast_to([P, ap.shape[1], n])
            then(nc.vector.tensor_reduce(best[:], g.gates[:], AX, ALU.max))
            then(nc.vector.tensor_tensor(cand[:], g.gates[:], wide(best[:], E), ALU.is_equal))
            then(nc.vector.tensor_scalar(cand[:], cand[:], -float(E), None, ALU.mult))
            then(nc.vector.tensor_tensor(cand[:], cand[:], by_token(expert), ALU.add))
            then(nc.vector.tensor_reduce(which[:], cand[:], AX, ALU.min))
            then(nc.vector.tensor_scalar(which[:], which[:], float(E), None, ALU.add))
            nc.vector.tensor_tensor(by_token(hot), by_token(expert), wide(which[:], E), ALU.is_equal).then_inc(hot_ready, 1)
            dve.wait_ge(hot_ready, 1)
            dve.wait_ge(counted, 1)
            then(nc.vector.tensor_copy(total[:].rearrange("p e t -> p (e t)"), count_ps[:, E * TT:]))
            flat = lambda t: t[:].rearrange("p e t -> p (e t)")
            then(nc.vector.tensor_tensor_scan(flat(upto), flat(run), flat(total), 0.0, ALU.mult, ALU.add))
            then(nc.vector.tensor_tensor(over[:], upto[:, :, TT - 1:TT].broadcast_to([P, E, FULL]), fills[:], ALU.is_gt))
            then(nc.vector.tensor_reduce(tiles[:], over[:], AX, ALU.add))
            then(nc.vector.tensor_tensor_scan(ends[:], ones[:, 0:E], tiles[:], 0.0, ALU.mult, ALU.add))
            then(nc.vector.tensor_tensor(before[:], ends[:], tiles[:], ALU.subtract))
            then(nc.vector.tensor_scalar(before[:], before[:], float(FT), None, ALU.mult))
            then(nc.vector.tensor_tensor(place[:], upto[:], total[:], ALU.subtract))
            then(nc.vector.tensor_tensor(place[:], place[:], wide(before[:], TT), ALU.add))
            then(nc.vector.tensor_tensor(flat(place), count_ps[:, 0:E * TT], flat(place), ALU.add))
            then(nc.vector.tensor_tensor(place[:], place[:], hot[:], ALU.mult))
            then(nc.vector.tensor_reduce(slot_f[:], place[:].rearrange("p e t -> p t e"), AX, ALU.add))
            nc.vector.tensor_copy(slot[:], slot_f[:]).then_inc(slot_ready, 1)
            then(nc.vector.tensor_tensor(passed[:], ends[:].rearrange("p (o e) -> p o e", o=1).broadcast_to([P, FFN_TILES, E]), tile_no[:], ALU.is_le))
            then(nc.vector.tensor_reduce(experts_f[:], passed[:], AX, ALU.add))
            then(nc.vector.tensor_scalar(experts_f[:], experts_f[:], float(E - 1), None, ALU.min))
            then(nc.vector.tensor_copy(g.tile_expert[:], experts_f[:]))

        @block.gpsimd
        def _(pool):
            pool.wait_ge(rows_ready, 2)
            pool.wait_ge(slot_ready, 1)
            pool.wait_ge(chain, 1)
            for t in range(TT):
                pool.indirect_dma_start(g.slots_dram, bass.IndirectOffsetOnAxis(ap=slot[:, t:t + 1], axis=0),
                                        rows[:, t, :], None).then_inc(scattered, 16)
            pool.wait_ge(scattered, 16 * TT)


def experts(nc, g):
    with ExitStack() as ctx:
        sb = lambda name, shape, dt=F32: ctx.enter_context(nc.sbuf_tensor(name, shape, dt))
        sem = lambda name: ctx.enter_context(nc.semaphore(name))
        NC = len(CHUNKS)
        S = 3
        w1, w2 = sb("w1", [C, S, 2, F]), sb("w2", [C, S, 2, F])
        w3 = sb("w3", [FC, S, NC, D])
        rows = sb("slot_rows", [P, S, 2, ROW])
        tt = sb("slot_t", [C, S, 2 * FT])
        act_sb = sb("silu", [FC, 2, FT])
        hid = sb("hidden", [FC, S, NC, FT])
        y = sb("y", [P, S, 2, D])
        psum = lambda name, shape: ctx.enter_context(nc.psum_tensor(name, shape, F32))
        t_ps = psum("slot_ps", [C, 2 * FT])
        h_ps = [psum(f"hid_ps{i}", [FC, 2 * FT]) for i in range(4)]
        y_ps = psum("y_ps", [P, HALF])

        w_loaded = [sem(f"w_loaded{j}") for j in range(S)]
        rows_loaded = [sem(f"rows_loaded{j}") for j in range(S)]
        t_ready, t_copied = sem("slot_t_ready"), sem("slot_t_copied")
        h_ready, silu_done, hid_done = sem("h_ready"), sem("silu_done"), sem("hid_done")
        y_ready, y_added = sem("y_ready"), sem("y_added")
        store_turn = sem("store_turn")
        y_stored = [sem(f"y_stored{j}") for j in range(S)]
        block = ctx.enter_context(nc.Block())
        N_T = FFN_TILES

        @block.sync
        def _(sp):
            def load(s):
                j = s.slot
                if s.before(S):
                    sp.wait_ge(y_ready, s.n - S + 1)
                e = sp.value_load(g.tile_expert[0:1, bass.ds(s.n, 1)], min_val=0, max_val=EXPERTS - 1)
                for dst, src in ((w1, g.w1_t), (w2, g.w2_t)):
                    sp.dma_start(dst[:, j], src[bass.ds(e, 1)].rearrange("o (c k) f -> k (o c) f", c=2)).then_inc(w_loaded[j], 16)
                full = (NC - 1) * FC
                w3_e = g.w3_t[bass.ds(e, 1)]
                sp.dma_start(w3[:, j, 0:NC - 1, :], w3_e[:, 0:full, :].rearrange("o (c k) d -> k (o c) d", k=FC)).then_inc(w_loaded[j], 16)
                sp.dma_start(w3[0:F - full, j, NC - 1:NC, :], w3_e[:, full:F, :].rearrange("o k d -> k o d")).then_inc(w_loaded[j], 16)
                if s.before(S):
                    sp.wait_ge(y_stored[j], 32 * s.group)
                sp.dma_start(rows[:, j], g.slots_dram[bass.ds(s.n * FT, FT), :].rearrange("(i p) d -> p i d", p=P)).then_inc(rows_loaded[j], 16)

            steps(sp, N_T, S, load)

        @block.gpsimd
        def _(pool):
            last_row = pool.to_reg(T - 1)

            def store(s):
                j = s.slot
                pool.wait_ge(y_added, s.n + 1)
                pool.sem_inc(store_turn, 1)
                for i in range(2):
                    pool.indirect_dma_start(g.out_rows, bass.IndirectOffsetOnAxis(ap=rows[:, j, i, 2 * D:ROW].bitcast(U32), axis=0),
                                            y[:, j, i, :], None, bounds_check=last_row, oob_is_err=False).then_inc(y_stored[j], 16)

            steps(pool, N_T, S, store)
            for j in range(S):
                pool.wait_ge(y_stored[j], 32 * ((N_T - j + S - 1) // S))

        @block.tensor
        def _(pe):
            def transposes(n, group, j, reused):
                pe.wait_ge(rows_loaded[j], 16 * (group + 1))
                if reused:
                    pe.wait_ge(t_copied, n)
                for c in range(2):
                    for i in range(2):
                        last = nc.tensor.transpose(t_ps[:, c * FT + i * P:c * FT + (i + 1) * P], rows[:, j, i, c * C:(c + 1) * C], g.ident[:])
                last.then_inc(t_ready, 1)

            def hidden(s, k):
                j = s.slot
                at, size = CHUNKS[k]
                if s.before(1):
                    pe.wait_ge(hid_done, NC * s.n + k - NC + 1)
                for h, w in enumerate((w1, w2)):
                    for c in range(2):
                        last = nc.tensor.matmul(h_ps[k][0:size, h * FT:(h + 1) * FT], w[:, j, c, at:at + size],
                                                tt[:, j, c * FT:(c + 1) * FT], start=(c == 0), stop=(c == 1), skip_group_check=True)
                last.then_inc(h_ready, 1)

            def output(n, j, reused):
                if reused:
                    pe.wait_ge(y_added, n)
                for k, (at, size) in enumerate(CHUNKS):
                    pe.wait_ge(hid_done, NC * n + k + 1)
                for i in range(2):
                    for k, (at, size) in enumerate(CHUNKS):
                        last = nc.tensor.matmul(y_ps[:, i * D:(i + 1) * D], hid[0:size, j, k, i * P:(i + 1) * P], w3[0:size, j, k, :],
                                                start=(k == 0), stop=(k == NC - 1))
                last.then_inc(y_ready, 1)

            transposes(0, 0, 0, False)

            def step(s):
                j = s.slot
                pe.wait_ge(w_loaded[j], 64 * (s.group + 1))
                pe.wait_ge(t_copied, s.n + 1)
                hidden(s, 0)
                if s.before(1):
                    output(s.n - 1, (j - 1) % S, s.before(2))
                for k in range(1, NC):
                    hidden(s, k)
                if s.after(1):
                    transposes(s.n + 1, s.group + (j + 1) // S, (j + 1) % S, True)

            steps(pe, N_T, S, step)
            output(N_T - 1, (N_T - 1) % S, True)

        @block.scalar
        def _(act):
            def copy_t(n, j, reused):
                act.wait_ge(t_ready, n + 1)
                if reused:
                    act.wait_ge(h_ready, NC * (n - S + 1))
                nc.scalar.activation(tt[:, j, :], t_ps[:], ACT.Copy).then_inc(t_copied, 1)

            copy_t(0, 0, False)

            def step(s):
                for k, (at, size) in enumerate(CHUNKS):
                    act.wait_ge(h_ready, NC * s.n + k + 1)
                    if s.before(1) or k >= 2:
                        act.wait_ge(hid_done, NC * s.n + k - 1)
                    nc.scalar.activation(act_sb[0:size, k % 2, :], h_ps[k][0:size, 0:FT], ACT.Silu).then_inc(silu_done, 1)
                if s.after(1):
                    copy_t(s.n + 1, (s.slot + 1) % S, s.before(2))

            steps(act, N_T, S, step)

        @block.vector
        def _(dve):
            def add_residual(n, j):
                dve.wait_ge(y_ready, n + 1)
                nc.vector.tensor_tensor(y[:, j], y_ps[:, 0:2 * D].rearrange("p (i d) -> p i d", i=2), rows[:, j, :, D:2 * D], ALU.add).then_inc(y_added, 1)

            def step(s):
                for k, (at, size) in enumerate(CHUNKS):
                    dve.wait_ge(silu_done, NC * s.n + k + 1)
                    if s.before(S):
                        dve.wait_ge(y_ready, s.n - S + 1)
                    nc.vector.tensor_tensor(hid[0:size, s.slot, k, :], h_ps[k][0:size, FT:2 * FT], act_sb[0:size, k % 2, :], ALU.mult).then_inc(hid_done, 1)
                    if k == 0 and s.before(1):
                        back = (s.slot - 1) % S
                        add_residual(s.n - 1, back)

            steps(dve, N_T, S, step)
            add_residual(N_T - 1, (N_T - 1) % S)


def key_rows():
    import numpy as np
    r = np.arange(HS)
    tile, row, col = np.meshgrid(np.arange(KT), np.arange(P // HS), np.arange(HS), indexing="ij")
    row = (tile % 2 * (P // HS) + row).reshape(1, N)
    col = col.reshape(1, N)
    hot = np.concatenate([row == r[:, None], col == r[:, None]])
    return np.concatenate([hot, hot, np.ones((1, N), bool)]).astype(np.float16)


def constants():
    import numpy as np
    f = np.float32
    E = EXPERTS
    every = lambda a: np.ascontiguousarray(np.broadcast_to(a.astype(f), (P,) + a.shape))
    return {
        "ident": np.eye(P, dtype=f),
        "low_rows": (np.arange(4 * HD) // HD % 2).astype(f)[:, None],
        "key_rows": key_rows(),
        "fold": np.tile(np.eye(4 * HD, dtype=f), (2, 1)),
        "tri": np.triu(np.ones((P, P), f), 1),
        "ones": np.ones((P, P), f),
        "expert": every(np.repeat(np.arange(E)[:, None], TT, 1)),
        "run": every(np.repeat(np.arange(TT)[None] > 0, E, 0)),
        "fills": every(np.repeat(np.arange(T // FT)[None] * FT, E, 0)),
        "tile_no": every(np.repeat(np.arange(FFN_TILES)[:, None], E, 1)),
        "token": (np.arange(P)[:, None] + P * np.arange(TT)[None]).astype(np.uint32),
        "empty_row": np.full((P, 1), T, np.uint32),
    }


def build(nc, ins, out):
    g = Shared()
    g.ident_dram, g.low_rows_dram, g.key_rows_dram, g.fold_dram = ins["ident"], ins["low_rows"], ins["key_rows"], ins["fold"]
    g.tri_dram, g.ones_dram, g.expert_dram, g.run_dram = ins["tri"], ins["ones"], ins["expert"], ins["run"]
    g.fills_dram, g.tile_no_dram, g.token_dram, g.empty_row_dram = ins["fills"], ins["tile_no"], ins["token"], ins["empty_row"]
    g.x_tiles = ins["x"].rearrange("(t p) d -> p t d", p=P)
    g.qkv_wt, g.qkv_b, g.rel_tables = ins["qkv_wt"], ins["qkv_b"], [ins["rel_h"], ins["rel_w"]]
    g.proj_wt, g.proj_b, g.gate_wt, g.gate_b = ins["proj_wt"], ins["proj_b"], ins["gate_wt"], ins["gate_b"]
    g.w1_t, g.w2_t, g.w3_t = ins["w1_t"], ins["w2_t"], ins["w3_t"]
    g.out_rows = out
    g.qk_split = nc.dram_tensor("qk_split", [2, 2, B * D, N], F16, kind="Internal").ap()
    g.qk_heads = g.qk_split.rearrange("k s (b h r) n -> k s h r b n", b=B, h=HEADS)
    g.rel_split = nc.dram_tensor("rel_split", [2, 2, B, HEADS, H, N], F16, kind="Internal").ap()
    g.rel_pairs = g.rel_split.rearrange("a s b h r n -> a s (b h) r n")
    g.slots_dram = nc.dram_tensor("slots", [SLOTS_ALL, ROW], F32, kind="Internal").ap()
    with ExitStack() as ctx:
        sb = lambda name, shape, dt=F32: ctx.enter_context(nc.sbuf_tensor(name, shape, dt))
        g.ident = sb("ident_sb", [P, P])
        g.x_sb = sb("x_sb", [P, TT, D])
        g.v_sb = sb("v_sb", [P, BH, KT, VW])
        g.att_sb = sb("att_sb", [P, BH, KT, HD])
        g.t_sb = sb("t_sb", [P, TT, D])
        g.gates = sb("gates_sb", [P, TT, EXPERTS])
        g.tile_expert = sb("tile_expert", [P, FFN_TILES], I32)
        project(nc, g)
        relative_positions(nc, g)
        attention(nc, g)
        gate(nc, g)
        route(nc, g)
        experts(nc, g)


def kernel(x, L0_conv_qkv_w, L0_conv_qkv_b, L0_conv_proj_w, L0_conv_proj_b, L0_conv_rel_pos_h, L0_conv_rel_pos_w,
           L0_ffn_Wg, L0_ffn_bg, L0_ffn_W1, L0_ffn_W2, L0_ffn_W3):
    import numpy as np
    import concourse.bacc as bacc
    from concourse.bass_utils import run_bass_kernel_spmd

    turned = lambda a: np.ascontiguousarray(np.swapaxes(np.asarray(a), -1, -2))
    row = lambda a: np.asarray(a).reshape(1, -1)
    arrays = {
        "x": np.asarray(x).reshape(T, D),
        "qkv_wt": turned(L0_conv_qkv_w), "qkv_b": row(L0_conv_qkv_b),
        "proj_wt": turned(L0_conv_proj_w), "proj_b": row(L0_conv_proj_b),
        "rel_h": turned(np.asarray(L0_conv_rel_pos_h)[::-1]), "rel_w": turned(np.asarray(L0_conv_rel_pos_w)[::-1]),
        "gate_wt": turned(L0_ffn_Wg), "gate_b": row(L0_ffn_bg),
        "w1_t": turned(L0_ffn_W1), "w2_t": turned(L0_ffn_W2), "w3_t": turned(L0_ffn_W3),
        **constants(),
    }
    nc = bacc.Bacc("TRN2", target_bir_lowering=False, num_devices=1)
    ins = {name: nc.dram_tensor(f"in_{name}", a.shape, mybir.dt.from_np(a.dtype), kind="ExternalInput").ap()
           for name, a in arrays.items()}
    out = nc.dram_tensor("out", [T, D], F32, kind="ExternalOutput").ap()
    build(nc, ins, out)
    result = run_bass_kernel_spmd(nc, [{f"in_{name}": a for name, a in arrays.items()}], core_ids=[0])
    return result.results[0]["out"].reshape(B, H, W, D)
```

```python
from contextlib import ExitStack

import concourse.bass as bass
from concourse import mybir

F32 = mybir.dt.float32
F16 = mybir.dt.float16
I32 = mybir.dt.int32
U32 = mybir.dt.uint32
ALU = mybir.AluOpType
ACT = mybir.ActivationFunctionType
AX = mybir.AxisListType.X

P = 128
B, H, W, D = 4, 32, 32, 192
HEADS, HD = 12, 16
N = H * W
T = B * N
TT = T // P
C = D // 2
BH = B * HEADS
HALF = 512
STEPS = T // HALF
TPS = HALF // P
HS = H // 2
KT = N // P
VW = HD + 1
SCALE = HD ** -0.5
EPS_ATT, EPS_FFN = 1e-6, 1e-5


class Shared:
    pass


class Step:

    def __init__(self, n, group, slot, total, known):
        self.n, self.group, self.slot, self.total, self.known = n, group, slot, total, known

    def before(self, k):
        return not self.known or self.n >= k

    def after(self, k):
        return not self.known or self.n + k < self.total


def steps(engine, total, unroll, body):
    groups = total // unroll
    for j in range(unroll):
        body(Step(j, 0, j, total, True))
    if groups > 2:
        with engine.Fori(1, groups - 1) as g:
            for j in range(unroll):
                body(Step(unroll * g + j, g, j, total, False))
    for n in range(max(unroll, unroll * (groups - 1)), total):
        body(Step(n, n // unroll, n % unroll, total, True))


def by_key(half):
    return half.rearrange("p (r i w) -> p i r w", i=2, w=HS)


def as_keys(half):
    return half.rearrange("p (i r w) -> p i r w", i=2, w=HS)


def project(nc, g):
    with ExitStack() as ctx:
        sb = lambda name, shape, dt=F32: ctx.enter_context(nc.sbuf_tensor(name, shape, dt))
        sem = lambda name: ctx.enter_context(nc.semaphore(name))
        w = [sb("qkv_w_top", [C, 3 * D]), sb("qkv_w_bottom", [C + 1, 3 * D])]
        stats = sb("stats", [P, TT, 6])
        mean = sb("mean", [P, TT])
        var, rstd, tmp = sb("var", [P, TT]), sb("rstd", [P, TT]), sb("tmp", [P, TT])
        xn = sb("xn", [P, 2, TPS, D])
        xt = [sb("xt_top", [C, 2, HALF]), sb("xt_bottom", [C + 1, 2, HALF])]
        hi = sb("qk_hi", [C, 2, 4, HALF], F16)
        lo = sb("qk_lo", [C, 2, 4, HALF], F16)
        psum = lambda name, shape: ctx.enter_context(nc.psum_tensor(name, shape, F32))
        t_ps = [psum(f"xt_ps{c}", [C, HALF]) for c in range(2)]
        qk_ps = [psum(f"qk_ps{m}", [C, HALF]) for m in range(4)]
        v_ps = [psum(f"v_ps{i}", [P, HALF]) for i in range(2)]

        x_loaded = [sem(f"x_loaded{c}") for c in range(4)]
        consts_loaded = sem("consts_loaded")
        stats_done, chain, root, root_done = sem("stats_done"), sem("att_chain"), sem("att_root"), sem("att_root_done")
        wk_scaled, ones_set = sem("wk_scaled"), sem("ones_set")
        rows_zeroed, table_loaded = sem("rows_zeroed"), sem("table_loaded")
        xn_ready, xt_ps_ready, xt_ready = sem("xn_ready"), sem("xt_ps_ready"), sem("xt_ready")
        qk_ready = sem("qk_ready")
        hi_done, lo_done = sem("hi_done"), sem("lo_done")
        v_ready, v_copied = sem("v_ready"), sem("v_copied")
        hi_stored = [sem(f"hi_stored{j}") for j in range(2)]
        lo_stored = [sem(f"lo_stored{j}") for j in range(2)]

        block = ctx.enter_context(nc.Block())
        XC = TT // 4

        @block.sync
        def _(sp):
            sp.dma_start(g.x_sb[:, 0:XC, :], g.x_tiles[:, 0:XC, :]).then_inc(x_loaded[0], 16)
            sp.dma_start(w[0][:], g.qkv_wt[0:C, :]).then_inc(consts_loaded, 16)
            sp.dma_start(w[1][0:C, :], g.qkv_wt[C:D, :]).then_inc(consts_loaded, 16)
            sp.dma_start(w[1][C:C + 1, :], g.qkv_b).then_inc(consts_loaded, 16)
            sp.dma_start(g.ident[:], g.ident_dram).then_inc(consts_loaded, 16)
            for c in range(1, 4):
                sp.dma_start(g.x_sb[:, c * XC:(c + 1) * XC, :], g.x_tiles[:, c * XC:(c + 1) * XC, :]).then_inc(x_loaded[c], 16)

            def store(s):
                for part, (src, done, stored) in enumerate(((hi, hi_done, hi_stored), (lo, lo_done, lo_stored))):
                    sp.wait_ge(done, 4 * s.n + 4)
                    for m in range(4):
                        dst = g.qk_split[m // 2, part, bass.ds(s.group * D + m % 2 * C, C), s.slot * HALF:(s.slot + 1) * HALF]
                        sp.dma_start(dst, src[:, s.slot, m, :]).then_inc(stored[s.slot], 16)

            steps(sp, STEPS, 2, store)
            for j in range(2):
                sp.wait_ge(hi_stored[j], 64 * (STEPS // 2))
                sp.wait_ge(lo_stored[j], 64 * (STEPS // 2))

        @block.gpsimd
        def _(pool):
            nc.gpsimd.memset(xt[1][C:C + 1, :, :], 1.0).then_inc(ones_set, 1)
            pool.wait_ge(ones_set, 1)
            nc.gpsimd.memset(g.v_sb[:], 1.0).then_inc(ones_set, 1)
            pool.wait_ge(ones_set, 2)
            nc.gpsimd.memset(g.slot_rows[:], 0.0).then_inc(rows_zeroed, 1)
            pool.wait_ge(rows_zeroed, 1)
            R = 2 * H - 1
            for r in range(4):
                for axis in range(2):
                    pool.dma_start(g.table[r * HD:(r + 1) * HD, axis * R:(axis + 1) * R], g.rel_tables[axis]).then_inc(table_loaded, 16)
            pool.dma_start(g.low_rows[:], g.low_rows_dram).then_inc(table_loaded, 16)
            pool.wait_ge(table_loaded, 16 * 9)

        @block.vector
        def _(dve):
            def statistics(chunks, calls):
                for c in chunks:
                    dve.wait_ge(x_loaded[c], 16)
                    for t in range(c * XC, (c + 1) * XC):
                        nc.vector.bn_stats(stats[:, t, :], g.x_sb[:, t, :]).then_inc(stats_done, 1)
                dve.wait_ge(stats_done, (chunks[-1] + 1) * XC)
                inverse_root(nc, dve, stats, mean, var, rstd, tmp, EPS_ATT, chain, root, root_done,
                             slice(chunks[0] * XC, (chunks[-1] + 1) * XC), calls)

            statistics([0], 0)
            dve.wait_ge(consts_loaded, 64)
            for half in w:
                nc.vector.tensor_scalar(half[:, D:2 * D], half[:, D:2 * D], SCALE, None, ALU.mult).then_inc(wk_scaled, 1)

            def normalize(n, slot, reused):
                if reused:
                    dve.wait_ge(xt_ps_ready, 2 * n - 2)
                for i in range(TPS):
                    t = n * TPS + i
                    nc.vector.tensor_scalar(xn[:, slot, i, :], g.x_sb[:, t, :], mean[:, bass.ds(t, 1)], rstd[:, bass.ds(t, 1)],
                                            ALU.subtract, ALU.mult).then_inc(xn_ready, 1)

            normalize(0, 0, False)
            normalize(1, 1, False)
            statistics([1, 2, 3], 1)

            def step(s):
                if s.after(1) and s.before(1):
                    normalize(s.n + 1, 1 - s.slot, True)
                if s.before(2):
                    dve.wait_ge(lo_stored[s.slot], 64 * s.group)
                for m in range(4):
                    dve.wait_ge(hi_done, 4 * s.n + m + 1)
                    nc.vector.tensor_tensor(lo[:, s.slot, m, :], qk_ps[m][:], hi[:, s.slot, m, :], ALU.subtract).then_inc(lo_done, 1)

            steps(dve, STEPS, 2, step)

        @block.scalar
        def _(act):
            for call, tiles in enumerate((slice(0, XC), slice(XC, TT))):
                act.wait_ge(root, call + 1)
                nc.scalar.activation(rstd[:, tiles], var[:, tiles], ACT.Sqrt).then_inc(root_done, 1)

            def step(s):
                for c in range(2):
                    act.wait_ge(xt_ps_ready, 2 * s.n + c + 1)
                    if s.before(2):
                        act.wait_ge(v_ready, 2 * s.n - 2)
                    nc.scalar.activation(as_keys(xt[c][0:C, s.slot, :]), by_key(t_ps[c][:]), ACT.Copy).then_inc(xt_ready, 1)
                if s.before(2):
                    act.wait_ge(hi_stored[s.slot], 64 * s.group)
                    act.wait_ge(lo_done, 4 * s.n - 4)
                for m in range(4):
                    act.wait_ge(qk_ready, 4 * s.n + m + 1)
                    nc.scalar.activation(hi[:, s.slot, m, :], qk_ps[m][:], ACT.Copy).then_inc(hi_done, 1)
                if s.n == 0 if s.known else False:
                    act.wait_ge(ones_set, 2)
                for i in range(2):
                    act.wait_ge(v_ready, 2 * s.n + i + 1)
                    tiles = g.v_sb[:, bass.ds(s.group * HEADS, HEADS), s.slot * 4 + 2 * i:s.slot * 4 + 2 * i + 2, 0:HD]
                    nc.scalar.activation(tiles.rearrange("p h t d -> p t h d"),
                                         v_ps[i][:, 0:2 * D].rearrange("p (t h d) -> p t h d", t=2, h=HEADS),
                                         ACT.Copy).then_inc(v_copied, 1)

            steps(act, STEPS, 2, step)

        @block.tensor
        def _(pe):
            pe.wait_ge(consts_loaded, 64)
            pe.wait_ge(wk_scaled, 2)
            pe.wait_ge(ones_set, 2)

            def step(s):
                pe.wait_ge(xn_ready, TPS * s.n + TPS)
                for c in range(2):
                    if s.before(1):
                        pe.wait_ge(xt_ready, 2 * s.n)
                    for i in range(TPS):
                        last = nc.tensor.transpose(t_ps[c][:, i * P:(i + 1) * P], xn[:, s.slot, i, c * C:(c + 1) * C], g.ident[:])
                    last.then_inc(xt_ps_ready, 1)
                pe.wait_ge(xt_ready, 2 * s.n + 2)
                for m in range(4):
                    if s.before(1):
                        pe.wait_ge(lo_done, 4 * s.n + m - 3)
                    for c in range(2):
                        tokens = xt[c][:, s.slot, :]
                        if m < 2:
                            tokens = tokens.rearrange("p (i r w) -> p r i w", i=2, w=HS)
                        last = nc.tensor.matmul(qk_ps[m][:], w[c][:, m * C:(m + 1) * C], tokens,
                                                start=(c == 0), stop=(c == 1))
                    last.then_inc(qk_ready, 1)
                for i in range(2):
                    if s.before(1):
                        pe.wait_ge(v_copied, 2 * s.n + i - 1)
                    for t in range(2):
                        for c in range(2):
                            keys = xt[c][:, s.slot, (2 * i + t) * P:(2 * i + t + 1) * P]
                            last = nc.tensor.matmul(v_ps[i][:, t * D:(t + 1) * D], keys, w[c][:, 2 * D:3 * D],
                                                    start=(c == 0), stop=(c == 1))
                    last.then_inc(v_ready, 1)

            steps(pe, STEPS, 2, step)


def fill(sp, g, n, head, slot):
    q, k, inc = g.q_side[slot], g.k_side[slot], g.loaded[slot]
    both = lambda ap: ap.rearrange("r (o n) -> r o n", o=1).broadcast_to([ap.shape[0], 4, N])
    q_hi, q_lo, k_hi, k_lo = (g.qk_split[i, part, bass.ds(slot * D + head * HD, HD), :] for i in range(2) for part in range(2))
    for at, src in ((0, q_hi), (HD, q_hi), (2 * HD, q_lo)):
        sp.dma_start(q[at:at + HD, :, :], both(src)).then_inc(inc, 16)
    for at, src in ((0, k_hi), (HD, k_lo), (2 * HD, k_hi)):
        sp.dma_start(k[at:at + HD, :], src).then_inc(inc, 16)
    for part in range(2):
        for axis in range(2):
            at = 3 * HD + (2 * part + axis) * HS
            halves = g.rel_pairs[axis, part, n].rearrange("(a r) n -> r a n", a=2)
            dst = q[at:at + HS, :, :].rearrange("p (i j) n -> p i j n", i=2)
            for other in range(2):
                where = dst[:, :, other, :] if axis == 0 else dst[:, other, :, :]
                sp.dma_start(where, halves).then_inc(inc, 16)


def relative_positions(nc, g):
    Q_ROWS = 4 * HD
    R = 2 * H - 1
    PAIRS = HEADS // 2
    FILL_AT = (1, PAIRS - 2, PAIRS - 1)
    with ExitStack() as ctx:
        sb = lambda name, shape, dt=F32: ctx.enter_context(nc.sbuf_tensor(name, shape, dt))
        sem = lambda name: ctx.enter_context(nc.semaphore(name))
        table, low_rows = g.table, g.low_rows
        table_hi = sb("table_hi", [Q_ROWS, 2 * R], F16)
        table_masked = sb("table_masked", [Q_ROWS, 2 * R])
        table_parts = sb("table_parts", [Q_ROWS, 2 * R], F16)
        q = sb("q_stack", [Q_ROWS, 2, 2, B, N], F16)
        hi = sb("rel_hi", [P, 2, 2, N], F16)
        lo = sb("rel_lo", [P, 2, 2, N], F16)
        rel_ps = [ctx.enter_context(nc.psum_tensor(f"rel_ps{axis}", [P, 2 * N], F32)) for axis in range(2)]

        table_split = sem("table_split")
        q_loaded = [sem(f"q_loaded{j}") for j in range(2)]
        rel_ready, hi_done, lo_done = sem("rel_ready"), sem("rel_hi_done"), sem("rel_lo_done")
        hi_stored = [sem(f"rel_hi_stored{axis}") for axis in range(2)]
        lo_stored = [sem(f"rel_lo_stored{axis}") for axis in range(2)]
        block = ctx.enter_context(nc.Block())

        @block.gpsimd
        def _(pool):
            for j in range(B):
                pool.dma_start(g.k_side[j][3 * HD:, :], g.key_rows_dram).then_inc(g.att_consts_loaded, 16)
            pool.dma_start(g.fold[:], g.fold_dram).then_inc(g.att_consts_loaded, 16)

        @block.sync
        def _(sp):
            def load(n, slot):
                for h in range(2):
                    for r in range(4):
                        src = g.qk_heads[0, r // 2, 2 * n + h]
                        sp.dma_start(q[r * HD:(r + 1) * HD, slot, h, :, :], src).then_inc(q_loaded[slot], 16)

            load(0, 0)
            load(1, 1)

            def fill_ahead(n):
                for axis in range(2):
                    sp.wait_ge(hi_stored[axis], 16)
                    sp.wait_ge(lo_stored[axis], 16)
                fill(sp, g, n, 0, n)

            def store(s):
                for axis in range(2):
                    for part, (src, done, stored) in enumerate(((hi, hi_done, hi_stored), (lo, lo_done, lo_stored))):
                        sp.wait_ge(done, 2 * s.n + axis + 1)
                        sp.dma_start(g.rel_split[axis, part, bass.ds(2 * s.n, 2)].rearrange("h b r n -> (b r) h n"),
                                     src[:, axis, :, :]).then_inc(stored[axis], 16)
                if s.after(2):
                    load(s.n + 2, s.slot)
                if s.known and s.n in FILL_AT:
                    fill_ahead(FILL_AT.index(s.n))

            steps(sp, PAIRS, 2, store)
            for axis in range(2):
                sp.wait_ge(hi_stored[axis], 16 * PAIRS)
                sp.wait_ge(lo_stored[axis], 16 * PAIRS)

        @block.tensor
        def _(pe):
            pe.wait_ge(table_split, 3)

            def products(s):
                pe.wait_ge(q_loaded[s.slot], 128 * s.group + 128)
                for axis in range(2):
                    if s.before(1):
                        pe.wait_ge(lo_done, 2 * s.n + axis - 1)
                    for i in range(H):
                        rows = table_parts[:, axis * R + H - 1 - i:axis * R + 2 * H - 1 - i]
                        for b in range(B):
                            image = q[:, s.slot, :, b, :].rearrange("p h (r w) -> p h r w", w=W)
                            last = nc.tensor.matmul(rel_ps[axis][b * H:(b + 1) * H, i * 2 * W:(i + 1) * 2 * W], rows,
                                                    image[:, :, i, :] if axis == 0 else image[:, :, :, i], start=True, stop=True)
                    last.then_inc(rel_ready, 1)

            steps(pe, PAIRS, 2, products)

        def product(axis, h):
            return rel_ps[axis][:].rearrange("p (i h j) -> p h i j", h=2, j=W)[:, h]

        def by_query(part, axis, h):
            return part[:, axis, h, :].rearrange("p (r w) -> p r w" if axis == 0 else "p (r w) -> p w r", w=W)

        @block.scalar
        def _(act):
            nc.scalar.activation(table_hi[:], table[:], ACT.Copy).then_inc(table_split, 1)

            def high_parts(s):
                for axis in range(2):
                    act.wait_ge(rel_ready, 2 * s.n + axis + 1)
                    if s.before(1):
                        act.wait_ge(hi_stored[axis], 16 * s.n)
                        act.wait_ge(lo_done, 2 * s.n + axis - 1)
                    for h in range(2):
                        last = nc.scalar.activation(by_query(hi, axis, h), product(axis, h), ACT.Copy)
                    last.then_inc(hi_done, 1)

            steps(act, PAIRS, 2, high_parts)

        @block.vector
        def _(dve):
            dve.wait_ge(table_split, 1)
            nc.vector.tensor_scalar(table_masked[:], table_hi[:], low_rows[:], None, ALU.mult).then_inc(table_split, 1)
            dve.wait_ge(table_split, 2)
            nc.vector.tensor_tensor(table_parts[:], table[:], table_masked[:], ALU.subtract).then_inc(table_split, 1)

            def low_parts(s):
                for axis in range(2):
                    dve.wait_ge(hi_done, 2 * s.n + axis + 1)
                    if s.before(1):
                        dve.wait_ge(lo_stored[axis], 16 * s.n)
                    for h in range(2):
                        last = nc.vector.tensor_tensor(by_query(lo, axis, h), product(axis, h), by_query(hi, axis, h), ALU.subtract)
                    last.then_inc(lo_done, 1)

            steps(dve, PAIRS, 2, low_parts)


def attention(nc, g):
    QK_ROWS = 3 * HD
    REL_ROW = QK_ROWS
    MAX_ROW = QK_ROWS + 4 * HS
    ROWS = MAX_ROW + 1
    SLOTS = B
    QUARTERS = 4
    PAIR_TILES = KT // 2
    GROUP = 4
    RING = 2 * GROUP
    LOADS = 14
    with ExitStack() as ctx:
        sb = lambda name, shape, dt=F32: ctx.enter_context(nc.sbuf_tensor(name, shape, dt))
        sem = lambda name: ctx.enter_context(nc.semaphore(name))
        q_side, k_side, loaded, consts_loaded, fold = g.q_side, g.k_side, g.loaded, g.att_consts_loaded, g.fold
        values = [sb(f"values{j}", [P, KT, 2 * HD]) for j in range(SLOTS)]
        probs = sb("probs", [P, RING, HALF])
        neg_max = sb("neg_max", [P, 2, KT], F16)
        max_rows = sb("max_rows", [KT, 2, P], F16)
        ident16 = sb("ident16", [P, P], F16)
        out_t = sb("out_t", [P, HALF])
        recip = sb("recip", [P, KT])
        max_ps = [ctx.enter_context(nc.psum_tensor(f"max_ps{i}", [P, N], F32)) for i in range(2)]
        ring_ps = [ctx.enter_context(nc.psum_tensor(f"ring_ps{i}", [P, HALF], F32)) for i in range(3)]
        out_ps = ctx.enter_context(nc.psum_tensor("out_ps", [P, HALF], F32))
        MAX_AT, FOLD_AT, TURN = 8, 13, 18
        FOLDED = 4 * 4 * HD
        folded_sb = sb("folded", [P, FOLDED])

        def score_at(k):
            return k + (k >= 8) + (k >= 12)

        zeroed = sem("values_zeroed")
        ident_cast = sem("ident_cast")
        max_loaded = [sem(f"max_loaded{j}") for j in range(SLOTS)]
        values_ready = sem("values_ready")
        raw_ready, tile_max = sem("raw_ready"), sem("tile_max")
        max_t_ready, max_copied = sem("max_t_ready"), sem("max_copied")
        scores_ready, exp_done, group_done = sem("scores_ready"), sem("exp_done"), sem("group_done")
        out_copied, folded, fold_copied = sem("out_copied"), sem("fold_ready"), sem("fold_copied")
        recip_done, att_done = sem("recip_done"), sem("att_done")
        block = ctx.enter_context(nc.Block())

        @block.sync
        def _(sp):
            def store_max(n, slot):
                sp.wait_ge(max_copied, n + 1)
                for quarter in range(QUARTERS):
                    sp.dma_start(q_side[slot][MAX_ROW:ROWS, quarter, :].rearrange("o (t p) -> o t p", p=P),
                                 max_rows[:, slot % 2, :]).then_inc(max_loaded[slot], 16)

            store_max(0, 0)

            def step(s):
                if s.after(3):
                    if s.before(1):
                        sp.wait_ge(scores_ready, 16 * s.n)
                    fill(sp, g, s.n + 3, s.group + (s.slot + 3) // SLOTS, (s.slot + 3) % SLOTS)
                if s.after(1):
                    store_max(s.n + 1, (s.slot + 1) % SLOTS)

            steps(sp, BH, SLOTS, step)

        @block.gpsimd
        def _(pool):
            for j in range(SLOTS):
                nc.gpsimd.memset(values[j][:], 0.0).then_inc(zeroed, 1)
            pool.wait_ge(zeroed, SLOTS)

            def step(s):
                if s.before(4):
                    pool.wait_ge(group_done, PAIR_TILES * (s.n - SLOTS + 1))
                nc.gpsimd.tensor_copy(values[s.slot][:, :, 0:VW], g.v_sb[:, s.group + s.slot * HEADS]).then_inc(values_ready, 1)

            steps(pool, BH, SLOTS, step)

        @block.tensor
        def _(pe):
            pe.wait_ge(consts_loaded, 16 * (SLOTS + 1))
            pe.wait_ge(ident_cast, 1)

            def raw_scores(n, slot, t, reused):
                if reused:
                    pe.wait_ge(tile_max, KT * n + t - 1)
                for quarter in range(QUARTERS):
                    keys = slice(quarter * 2 * P, (quarter + 1) * 2 * P)
                    last = nc.tensor.matmul(max_ps[t % 2][:, keys], q_side[slot][0:MAX_ROW, quarter, t * P:(t + 1) * P],
                                            k_side[slot][0:MAX_ROW, keys], start=True, stop=True, skip_group_check=True)
                last.then_inc(raw_ready, 1)

            def bank_free(s, at):
                at -= 3
                back = 0
                while True:
                    if at < 0:
                        at, back = at + TURN, 1
                        if not s.before(1):
                            return
                    if at == MAX_AT and (back or s.after(1)):
                        return pe.wait_ge(max_copied, s.n - back + 2)
                    if at == FOLD_AT and (s.before(1) if not back else s.before(2)):
                        return pe.wait_ge(fold_copied, s.n - back)
                    if at not in (MAX_AT, FOLD_AT):
                        k = at - (at > MAX_AT) - (at > FOLD_AT)
                        return pe.wait_ge(exp_done, KT * 2 * (s.n - back) + k + 1)
                    at -= 3

            def transpose_max(n, slot):
                pe.wait_ge(tile_max, KT * (n + 1))
                nc.tensor.matmul(ring_ps[MAX_AT % 3][0:KT, 0:P], neg_max[:, slot % 2, :], ident16[:],
                                 start=True, stop=True).then_inc(max_t_ready, 1)

            def scores(s, u, i):
                tile, at = 2 * u + i // 2, score_at(GROUP * u + i)
                bank_free(s, at)
                nc.tensor.matmul(ring_ps[at % 3][:], k_side[s.slot][:, tile * P:(tile + 1) * P],
                                 q_side[s.slot][:, tile // 2, (i % 2) * HALF:(i % 2 + 1) * HALF],
                                 start=True, stop=True).then_inc(scores_ready, 1)

            def weighted_values(n, slot, u):
                pe.wait_ge(exp_done, 16 * n + GROUP * u + GROUP)
                for i in range(GROUP):
                    tile = 2 * u + i // 2
                    last = nc.tensor.matmul(out_ps[i * 2 * HD:(i + 1) * 2 * HD, :], values[slot][:, tile, :],
                                            probs[:, u % 2 * GROUP + i, :], start=(u == 0), stop=(u == PAIR_TILES - 1),
                                            tile_position=(0, i * 2 * HD))
                last.then_inc(group_done, 1)

            def fold_out(n):
                pe.wait_ge(out_copied, n + 1)
                for blk in range(4):
                    last = nc.tensor.matmul(ring_ps[FOLD_AT % 3][:, blk * 4 * HD:(blk + 1) * 4 * HD], out_t[:, blk * P:(blk + 1) * P],
                                            fold[:], start=True, stop=True, skip_group_check=True)
                last.then_inc(folded, 1)

            for n, tiles in ((0, KT), (1, 6)):
                pe.wait_ge(loaded[n], 16 * LOADS)
                for t in range(tiles):
                    raw_scores(n, n, t, KT * n + t >= 2)
                if n == 0:
                    transpose_max(0, 0)

            def step(s):
                j = s.slot
                one, two, back = (j + 1) % SLOTS, (j + 2) % SLOTS, (j - 1) % SLOTS
                for u in range(PAIR_TILES):
                    if u == 0:
                        pe.wait_ge(max_loaded[j], 64 * (s.group + 1))
                    if u == 1 and s.after(2):
                        pe.wait_ge(loaded[two], 16 * LOADS * (s.group + (2 if j >= 2 else 1)))
                    for i in range(GROUP):
                        scores(s, u, i)
                        if i in (1, 2):
                            if u == 0 and s.after(1):
                                raw_scores(s.n + 1, one, 6 + i - 1, True)
                            if u >= 1 and s.after(2):
                                raw_scores(s.n + 2, two, 2 * (u - 1) + i - 1, True)
                    if u == 0 and s.before(1):
                        weighted_values(s.n - 1, back, PAIR_TILES - 1)
                    if u == 1:
                        pe.wait_ge(values_ready, s.n + 1)
                        if s.before(1):
                            pe.wait_ge(out_copied, s.n)
                    if u >= 1:
                        weighted_values(s.n, j, u - 1)
                    if u == 1 and s.after(1):
                        bank_free(s, MAX_AT)
                        transpose_max(s.n + 1, one)
                    if u == 2 and s.before(1):
                        bank_free(s, FOLD_AT)
                        fold_out(s.n - 1)

            steps(pe, BH, SLOTS, step)
            weighted_values(BH - 1, (BH - 1) % SLOTS, PAIR_TILES - 1)
            pe.wait_ge(exp_done, 2 * KT * BH)
            fold_out(BH - 1)

        @block.scalar
        def _(act):
            nc.scalar.activation(ident16[:], g.ident[:], ACT.Copy).then_inc(ident_cast, 1)

            def copy_max(n, slot, fills):
                act.wait_ge(max_t_ready, n + 1)
                if fills is not None:
                    act.wait_ge(max_loaded[(slot - 2) % SLOTS], 64 * fills)
                nc.scalar.activation(max_rows[:, slot % 2, :], ring_ps[MAX_AT % 3][0:KT, 0:P], ACT.Copy).then_inc(max_copied, 1)

            def copy_out(n, reused):
                act.wait_ge(group_done, PAIR_TILES * (n + 1))
                if reused:
                    act.wait_ge(folded, n)
                nc.scalar.activation(out_t[:], out_ps[:], ACT.Copy).then_inc(out_copied, 1)

            def copy_fold(n, reused):
                act.wait_ge(folded, n + 1)
                if reused:
                    act.wait_ge(att_done, n)
                nc.scalar.activation(folded_sb[:], ring_ps[FOLD_AT % 3][:, 0:FOLDED], ACT.Copy).then_inc(fold_copied, 1)

            copy_max(0, 0, None)

            def step(s):
                for u in range(PAIR_TILES):
                    for i in range(GROUP):
                        if u == 1 and i == 2 and s.before(1):
                            copy_out(s.n - 1, s.before(2))
                        if i == 0 and (s.before(1) or u >= 2):
                            act.wait_ge(group_done, PAIR_TILES * s.n + u - 1)
                        act.wait_ge(scores_ready, 16 * s.n + GROUP * u + i + 1)
                        nc.scalar.activation(probs[:, u % 2 * GROUP + i, :], ring_ps[score_at(GROUP * u + i) % 3][:], ACT.Exp).then_inc(exp_done, 1)
                    if u == 1 and s.after(1):
                        one = (s.slot + 1) % SLOTS
                        earlier = None if not s.before(1) else (s.group + 1 if s.slot >= 1 else s.group)
                        copy_max(s.n + 1, one, earlier)
                    if u == 2 and s.before(1):
                        copy_fold(s.n - 1, s.before(2))

            steps(act, BH, SLOTS, step)
            copy_out(BH - 1, True)
            copy_fold(BH - 1, True)

        @block.vector
        def _(dve):
            def take_max(n, slot, t, reused):
                dve.wait_ge(raw_ready, KT * n + t + 1)
                if reused:
                    dve.wait_ge(max_t_ready, n - 1)
                nc.vector.tensor_reduce(neg_max[:, slot % 2, t:t + 1], max_ps[t % 2][:], AX, ALU.max, negate=True).then_inc(tile_max, 1)

            def normalize(n, head, image, reused):
                dve.wait_ge(fold_copied, n + 1)
                by_block = folded_sb[:].rearrange("p (b h c) -> p b h c", b=4, h=2)
                if reused:
                    dve.wait_ge(att_done, n)
                nc.vector.reciprocal(recip[:].rearrange("p (h b) -> p b h", h=2), by_block[:, :, :, HD]).then_inc(recip_done, 1)
                dve.wait_ge(recip_done, n + 1)
                dst = g.att_sb[:, head + image * HEADS].rearrange("p (h b) d -> p b h d", h=2)
                by = recip[:].rearrange("p (h b o) -> p b h o", h=2, o=1).broadcast_to([P, 4, 2, HD])
                nc.vector.tensor_tensor(dst, by_block[:, :, :, 0:HD], by, ALU.mult).then_inc(att_done, 1)

            for n, tiles in ((0, KT), (1, 6)):
                for t in range(tiles):
                    take_max(n, n, t, False)

            def step(s):
                for u in range(PAIR_TILES):
                    for i in range(2):
                        if u == 0 and s.after(1):
                            take_max(s.n + 1, s.slot + 1, 6 + i, False)
                        if u >= 1 and s.after(2):
                            take_max(s.n + 2, s.slot + 2, 2 * (u - 1) + i, u == 1 and i == 0)
                    if u == 2 and s.before(1):
                        normalize(s.n - 1, s.group + (s.slot - 1) // SLOTS, (s.slot - 1) % SLOTS, s.before(2))

            steps(dve, BH, SLOTS, step)
            normalize(BH - 1, HEADS - 1, B - 1, True)


FT = 128
EXPERTS, F = 8, 469
FC = 118
CHUNKS = [(c * FC, min(FC, F - c * FC)) for c in range(-(-F // FC))]
FFN_TILES = T // FT + EXPERTS - 1
SLOTS_ALL = FFN_TILES * FT
SG = SLOTS_ALL // P
TAIL = D - P
AT_TAIL, AT_X = D, D + TAIL
ROW = AT_X + D
S = 3


def gate(nc, g):
    with ExitStack() as ctx:
        sb = lambda name, shape, dt=F32: ctx.enter_context(nc.sbuf_tensor(name, shape, dt))
        sem = lambda name: ctx.enter_context(nc.semaphore(name))
        w = [sb("proj_w_top", [C, D]), sb("proj_w_bottom", [C + 1, D])]
        wg = [sb("gate_w_top", [C, EXPERTS]), sb("gate_w_bottom", [C + 1, EXPERTS])]
        att = sb("att", [P, 2, TPS, D])
        at = [sb("at_top", [C, 2, HALF]), sb("at_bottom", [C + 1, 2, HALF])]
        stats = sb("stats2", [P, TT, 6])
        mean = sb("mean2", [P, TT])
        var, rstd, tmp = sb("var2", [P, TT]), sb("rstd2", [P, TT]), sb("tmp2", [P, TT])
        tn = sb("tn", [P, 2, TPS, D])
        psum = lambda name, shape: ctx.enter_context(nc.psum_tensor(name, shape, F32))
        t_ps = [psum(f"at_ps{c}", [C, HALF]) for c in range(2)]
        p_ps = [psum(f"proj_ps{i}", [P, HALF]) for i in range(4)]
        g_ps = [psum(f"gate_ps{i}", [P, TPS * EXPERTS]) for i in range(2)]

        tables_loaded, experts_loaded = sem("tables_loaded"), sem("experts_loaded")
        loaded, ones_set, att_ready = sem("gate_loaded"), sem("gate_ones"), sem("att_ready")
        at_ps_ready, at_ready, proj_ready, x1_ready = sem("at_ps_ready"), sem("at_ready"), sem("proj_ready"), sem("x1_ready")
        stats_done, chain = sem("stats2_done"), sem("ffn_chain")
        root, root_done, tn_ready = sem("root"), sem("root_done"), sem("tn_ready")
        x1_stored, tn_stored = [[sem(f"{what}_stored{j}") for j in range(2)] for what in ("x1", "tn")]
        tt_ps_ready, tt_ready, gate_ready, gate_copied = sem("tt_ps_ready"), sem("tt_ready"), sem("gate_ready"), sem("gate_copied")
        block = ctx.enter_context(nc.Block())

        @block.sync
        def _(sp):
            sp.dma_start(w[0][:], g.proj_wt[0:C, :]).then_inc(loaded, 16)
            sp.dma_start(w[1][0:C, :], g.proj_wt[C:D, :]).then_inc(loaded, 16)
            sp.dma_start(w[1][C:C + 1, :], g.proj_b).then_inc(loaded, 16)
            sp.dma_start(wg[0][:], g.gate_wt[0:C, :]).then_inc(loaded, 16)
            sp.dma_start(wg[1][0:C, :], g.gate_wt[C:D, :]).then_inc(loaded, 16)
            sp.dma_start(wg[1][C:C + 1, :], g.gate_b).then_inc(loaded, 16)
            for name in ROUTE_TABLES:
                sp.dma_start(g.route_tables[name][:], g.route_dram[name]).then_inc(tables_loaded, 16)

            def store_residual(s):
                sp.wait_ge(x1_ready, 2 * s.n + 2)
                tiles = bass.ds(TPS * s.n, TPS)
                sp.dma_start(g.token_tiles[:, tiles, AT_X:ROW], g.x_sb[:, tiles, :]).then_inc(x1_stored[s.slot], 16)

            steps(sp, STEPS, 2, store_residual)

            def store_normalized(s):
                sp.wait_ge(tn_ready, TPS * s.n + TPS)
                rows = g.token_tiles[:, bass.ds(TPS * s.n, TPS), :]
                sp.dma_start(rows[:, :, 0:D], tn[:, s.slot]).then_inc(tn_stored[s.slot], 16)
                sp.dma_start(rows[:, :, AT_TAIL:AT_X], tn[:, s.slot, :, P:D]).then_inc(tn_stored[s.slot], 16)

            steps(sp, STEPS, 2, store_normalized)
            for j in range(2):
                sp.wait_ge(x1_stored[j], 16 * (STEPS // 2))
                sp.wait_ge(tn_stored[j], 32 * (STEPS // 2))
            sp.wait_ge(tables_loaded, 16 * len(ROUTE_TABLES))

        @block.gpsimd
        def _(pool):
            nc.gpsimd.memset(at[1][C:C + 1, :, :], 1.0).then_inc(ones_set, 1)
            pool.wait_ge(ones_set, 1)
            pool.wait_ge(loaded, 96)
            load_experts(pool, g, experts_loaded)

        @block.tensor
        def _(pe):
            pe.wait_ge(loaded, 96)
            pe.wait_ge(ones_set, 1)

            def transposes(src, slot, ready):
                for c in range(2):
                    for i in range(TPS):
                        last = nc.tensor.transpose(t_ps[c][:, i * P:(i + 1) * P], src[:, slot, i, c * C:(c + 1) * C], g.ident[:])
                    last.then_inc(ready, 1)

            pe.wait_ge(att_ready, 1)
            transposes(att, 0, at_ps_ready)

            def project_out(s):
                pe.wait_ge(at_ready, 2 * s.n + 2)
                if s.after(1):
                    pe.wait_ge(att_ready, s.n + 2)
                    transposes(att, 1 - s.slot, at_ps_ready)
                if s.before(2):
                    pe.wait_ge(x1_ready, 2 * s.n - 2)
                for i in range(TPS):
                    for c in range(2):
                        last = nc.tensor.matmul(p_ps[2 * s.slot + i // 2][:, i % 2 * D:(i % 2 + 1) * D],
                                                at[c][:, s.slot, i * P:(i + 1) * P], w[c][:], start=(c == 0), stop=(c == 1))
                    if i % 2:
                        last.then_inc(proj_ready, 1)

            steps(pe, STEPS, 2, project_out)

            pe.wait_ge(tn_ready, TPS)
            transposes(tn, 0, tt_ps_ready)

            def gates(s):
                pe.wait_ge(tt_ready, 2 * s.n + 2)
                if s.after(1):
                    pe.wait_ge(tn_ready, TPS * s.n + 2 * TPS)
                    transposes(tn, 1 - s.slot, tt_ps_ready)
                if s.before(2):
                    pe.wait_ge(gate_copied, s.n - 1)
                for i in range(TPS):
                    for c in range(2):
                        last = nc.tensor.matmul(g_ps[s.slot][:, i * EXPERTS:(i + 1) * EXPERTS], at[c][:, s.slot, i * P:(i + 1) * P],
                                                wg[c][:], start=(c == 0), stop=(c == 1))
                last.then_inc(gate_ready, 1)

            steps(pe, STEPS, 2, gates)

        @block.scalar
        def _(act):
            def gather_heads(n, head_group, slot, reused):
                if reused:
                    act.wait_ge(at_ps_ready, 2 * n - 2)
                src = g.att_sb[:, bass.ds(head_group * HEADS, HEADS), slot * TPS:(slot + 1) * TPS, :]
                nc.scalar.activation(att[:, slot].rearrange("p t (h d) -> p t h d", h=HEADS),
                                     src.rearrange("p h t d -> p t h d"), ACT.Copy).then_inc(att_ready, 1)

            gather_heads(0, 0, 0, False)

            def copy_at(s):
                if s.after(1):
                    gather_heads(s.n + 1, s.group + s.slot, 1 - s.slot, s.before(1))
                for c in range(2):
                    act.wait_ge(at_ps_ready, 2 * s.n + c + 1)
                    if s.before(2):
                        act.wait_ge(proj_ready, 2 * s.n - 2)
                    nc.scalar.activation(at[c][0:C, s.slot, :], t_ps[c][:], ACT.Copy).then_inc(at_ready, 1)

            steps(act, STEPS, 2, copy_at)
            act.wait_ge(root, 1)
            nc.scalar.activation(rstd[:], var[:], ACT.Sqrt).then_inc(root_done, 1)

            def copy_gates(n, slot):
                act.wait_ge(gate_ready, n + 1)
                nc.scalar.activation(g.gates[:, bass.ds(TPS * n, TPS), :], g_ps[slot][:], ACT.Copy).then_inc(gate_copied, 1)

            def copy_tt(s):
                for c in range(2):
                    act.wait_ge(tt_ps_ready, 2 * s.n + c + 1)
                    if s.before(2):
                        act.wait_ge(gate_ready, s.n - 1)
                    else:
                        act.wait_ge(proj_ready, 2 * STEPS)
                    nc.scalar.activation(at[c][0:C, s.slot, :], t_ps[c][:], ACT.Copy).then_inc(tt_ready, 1)
                if s.before(1):
                    copy_gates(s.n - 1, 1 - s.slot)

            steps(act, STEPS, 2, copy_tt)
            copy_gates(STEPS - 1, 1)

        @block.vector
        def _(dve):
            def residual(s):
                for i in range(2):
                    dve.wait_ge(proj_ready, 2 * s.n + i + 1)
                    x = g.x_sb[:, bass.ds(TPS * s.n + 2 * i, 2), :]
                    nc.vector.tensor_tensor(x, p_ps[2 * s.slot + i][:, 0:2 * D].rearrange("p (t d) -> p t d", t=2), x,
                                            ALU.add).then_inc(x1_ready, 1)
                for i in range(TPS):
                    dve.wait_ge(x1_ready, 2 * s.n + i // 2 + 1)
                    t = TPS * s.n + i
                    nc.vector.bn_stats(stats[:, t, :], g.x_sb[:, t, :]).then_inc(stats_done, 1)

            steps(dve, STEPS, 2, residual)
            dve.wait_ge(stats_done, TT)
            inverse_root(nc, dve, stats, mean, var, rstd, tmp, EPS_FFN, chain, root, root_done)

            def normalize(s):
                if s.before(2):
                    dve.wait_ge(tt_ps_ready, 2 * s.n - 2)
                    dve.wait_ge(tn_stored[s.slot], 32 * s.group)
                for i in range(TPS):
                    t = TPS * s.n + i
                    nc.vector.tensor_scalar(tn[:, s.slot, i, :], g.x_sb[:, t, :], mean[:, bass.ds(t, 1)], rstd[:, bass.ds(t, 1)],
                                            ALU.subtract, ALU.mult).then_inc(tn_ready, 1)

            steps(dve, STEPS, 2, normalize)


def load_experts(pool, g, loaded):
    NC, full = len(CHUNKS), (len(CHUNKS) - 1) * FC
    for h, src in enumerate((g.w1_t, g.w2_t)):
        by_channel = src.rearrange("e k f -> k e f")
        pool.dma_start(g.w_top[:, :, h, :], by_channel[0:P]).then_inc(loaded, 16)
        pool.dma_start(g.w_tail[h * TAIL:(h + 1) * TAIL, :, :], by_channel[P:D]).then_inc(loaded, 16)
    for e in range(EXPERTS):
        pool.dma_start(g.w3[:, e, 0:NC - 1, :], g.w3_t[e, 0:full, :].rearrange("(c k) d -> k c d", k=FC)).then_inc(loaded, 16)
    pool.dma_start(g.w3[0:F - full, :, NC - 1, :], g.w3_t[:, full:F, :].rearrange("e k d -> k e d")).then_inc(loaded, 16)
    pool.wait_ge(loaded, 16 * (4 + EXPERTS + 1))


def inverse_root(nc, dve, stats, mean, var, rstd, tmp, eps, chain, root, root_done, tiles=slice(0, TT), calls=0):
    LINKS = 12
    done = [LINKS * calls]
    stats, mean, var, rstd, tmp = stats[:, tiles, :], mean[:, tiles], var[:, tiles], rstd[:, tiles], tmp[:, tiles]

    def then(instruction):
        done[0] += 1
        instruction.then_inc(chain, 1)
        dve.wait_ge(chain, done[0])

    tt = nc.vector.tensor_tensor
    then(tt(tmp, stats[:, :, 1], stats[:, :, 4], ALU.subtract))
    then(tt(tmp, tmp, tmp, ALU.mult))
    then(tt(mean, stats[:, :, 1], stats[:, :, 4], ALU.add))
    then(nc.vector.tensor_scalar(mean, mean, 0.5, None, ALU.mult))
    then(tt(var, stats[:, :, 2], stats[:, :, 5], ALU.add))
    then(nc.vector.tensor_scalar(var, var, 1.0 / D, eps, ALU.mult, ALU.add))
    then(nc.vector.tensor_scalar(tmp, tmp, 0.25, None, ALU.mult))
    tt(var, var, tmp, ALU.add).then_inc(root, 1)
    dve.wait_ge(root, calls + 1)
    dve.wait_ge(root_done, calls + 1)
    then(nc.vector.reciprocal(rstd, rstd))
    then(tt(tmp, rstd, rstd, ALU.mult))
    then(tt(tmp, tmp, var, ALU.mult))
    then(nc.vector.tensor_scalar(tmp, tmp, -0.5, 1.5, ALU.mult, ALU.add))
    then(tt(rstd, rstd, tmp, ALU.mult))
    assert done[0] == LINKS * (calls + 1)


ROUTE_TABLES = {"tri": [P, P], "ones": [P, P], "expert": [P, EXPERTS, TT], "run": [P, EXPERTS, TT], "fills": [P, EXPERTS, T // FT],
                "tile_no": [P, FFN_TILES, EXPERTS], "group_no": [P, TT, SG], "lane_no": [P, P], "tile": [P, TT], "lane_of": [P, 1]}


def route(nc, g):
    E = EXPERTS
    FULL = T // FT
    LT = 8
    with ExitStack() as ctx:
        sb = lambda name, shape, dt=F32: ctx.enter_context(nc.sbuf_tensor(name, shape, dt))
        sem = lambda name: ctx.enter_context(nc.semaphore(name))
        tri, ones, expert, run, fills, tile_no, group_no, lane_no, tile, lane_of = (g.route_tables[name] for name in ROUTE_TABLES)
        best, which, hot, cand = sb("best", [P, TT]), sb("which", [P, TT]), sb("hot", [P, E, TT], F16), sb("cand", [P, TT, E])
        total, upto, place = sb("total", [P, E, TT]), sb("upto", [P, E, TT]), sb("place", [P, E, TT])
        over, tiles, ends, before = sb("over", [P, E, FULL]), sb("tiles", [P, E]), sb("ends", [P, E]), sb("before_", [P, E])
        passed, experts_f, slot_f, slot = sb("passed", [P, FFN_TILES, E]), sb("experts_f", [P, FFN_TILES]), sb("slot_f", [P, TT]), sb("slot", [P, TT], I32)
        group_i, group, lane = sb("group_i", [P, TT], I32), sb("group", [P, TT]), sb("lane", [P, TT])
        in_group, in_lane = sb("in_group", [P, TT, SG], F16), sb("in_lane", [P, TT, P], F16)
        by_group = sb("by_group", [P, TT, 2, SG], F16)
        found, vacant = sb("found", [P, SG]), sb("vacant", [P, SG])
        count_ps = ctx.enter_context(nc.psum_tensor("count_ps", [P, 2 * E * TT], F32))
        found_ps = ctx.enter_context(nc.psum_tensor("found_ps", [P, HALF], F32))

        chain, hot_ready, counted = sem("route_chain"), sem("hot_ready"), sem("counted")
        group_ready, group_scaled, placed, found_ready = sem("group_ready"), sem("group_scaled"), sem("placed"), sem("found_ready")
        block = ctx.enter_context(nc.Block())

        @block.tensor
        def _(pe):
            pe.wait_ge(hot_ready, 1)
            flat = hot[:].rearrange("p e t -> p (e t)")
            nc.tensor.matmul(count_ps[:, 0:E * TT], tri[:], flat, start=True, stop=True, skip_group_check=True)
            nc.tensor.matmul(count_ps[:, E * TT:], ones[:], flat, start=True, stop=True, skip_group_check=True).then_inc(counted, 1)
            pe.wait_ge(group_scaled, 2)
            for t in range(TT):
                if t % LT == 0:
                    pe.wait_ge(placed, t // LT + 1)
                last = nc.tensor.matmul(found_ps[:, 0:2 * SG], in_lane[:, t, :], by_group[:, t, :, :], start=(t == 0), stop=(t == TT - 1))
            last.then_inc(found_ready, 1)

        @block.scalar
        def _(act):
            act.wait_ge(group_ready, 1)
            nc.scalar.activation(by_group[:, :, 1, :], in_group[:], ACT.Copy, scale=lane_of[:]).then_inc(group_scaled, 1)

        @block.vector
        def _(dve):
            done = [0]

            def then(instruction):
                done[0] += 1
                instruction.then_inc(chain, 1)
                dve.wait_ge(chain, done[0])

            by_token = lambda table: table[:].rearrange("p e t -> p t e")
            wide = lambda ap, n: ap.rearrange("p (t o) -> p t o", o=1).broadcast_to([P, ap.shape[1], n])
            then(nc.vector.tensor_reduce(best[:], g.gates[:], AX, ALU.max))
            then(nc.vector.tensor_tensor(cand[:], g.gates[:], wide(best[:], E), ALU.is_equal))
            then(nc.vector.tensor_scalar(cand[:], cand[:], -float(E), None, ALU.mult))
            then(nc.vector.tensor_tensor(cand[:], cand[:], by_token(expert), ALU.add))
            then(nc.vector.tensor_reduce(which[:], cand[:], AX, ALU.min))
            then(nc.vector.tensor_scalar(which[:], which[:], float(E), None, ALU.add))
            nc.vector.tensor_tensor(by_token(hot), by_token(expert), wide(which[:], E), ALU.is_equal).then_inc(hot_ready, 1)
            dve.wait_ge(hot_ready, 1)
            dve.wait_ge(counted, 1)
            then(nc.vector.tensor_copy(total[:].rearrange("p e t -> p (e t)"), count_ps[:, E * TT:]))
            flat = lambda t: t[:].rearrange("p e t -> p (e t)")
            then(nc.vector.tensor_tensor_scan(flat(upto), flat(run), flat(total), 0.0, ALU.mult, ALU.add))
            then(nc.vector.tensor_tensor(over[:], upto[:, :, TT - 1:TT].broadcast_to([P, E, FULL]), fills[:], ALU.is_gt))
            then(nc.vector.tensor_reduce(tiles[:], over[:], AX, ALU.add))
            then(nc.vector.tensor_tensor_scan(ends[:], run[:, 0, 1:E + 1], tiles[:], 0.0, ALU.mult, ALU.add))
            then(nc.vector.tensor_tensor(before[:], ends[:], tiles[:], ALU.subtract))
            then(nc.vector.tensor_scalar(before[:], before[:], float(FT), None, ALU.mult))
            then(nc.vector.tensor_tensor(place[:], upto[:], total[:], ALU.subtract))
            then(nc.vector.tensor_tensor(place[:], place[:], wide(before[:], TT), ALU.add))
            then(nc.vector.tensor_tensor(flat(place), count_ps[:, 0:E * TT], flat(place), ALU.add))
            then(nc.vector.tensor_tensor(place[:], place[:], hot[:], ALU.mult))
            then(nc.vector.tensor_reduce(slot_f[:], place[:].rearrange("p e t -> p t e"), AX, ALU.add))
            then(nc.vector.tensor_copy(slot[:], slot_f[:]))
            then(nc.vector.tensor_scalar(group_i[:], slot[:], 7, None, ALU.logical_shift_right))
            then(nc.vector.tensor_copy(group[:], group_i[:]))
            then(nc.vector.scalar_tensor_tensor(lane[:], group[:], -float(P), slot_f[:], ALU.mult, ALU.add))
            nc.vector.tensor_tensor(in_group[:], group_no[:], wide(group[:], SG), ALU.is_equal).then_inc(group_ready, 1)
            dve.wait_ge(group_ready, 1)
            nc.vector.tensor_tensor(by_group[:, :, 0, :], in_group[:], wide(tile[:], SG), ALU.mult).then_inc(group_scaled, 1)
            for c in range(TT // LT):
                some = slice(c * LT, (c + 1) * LT)
                lanes = lane_no[:].rearrange("p (o n) -> p o n", o=1).broadcast_to([P, LT, P])
                nc.vector.tensor_tensor(in_lane[:, some, :], lanes, wide(lane[:, some], P), ALU.is_equal).then_inc(placed, 1)
            then(nc.vector.tensor_tensor(passed[:], ends[:].rearrange("p (o e) -> p o e", o=1).broadcast_to([P, FFN_TILES, E]), tile_no[:], ALU.is_le))
            then(nc.vector.tensor_reduce(experts_f[:], passed[:], AX, ALU.add))
            then(nc.vector.tensor_scalar(experts_f[:], experts_f[:], float(E - 1), None, ALU.min))
            then(nc.vector.tensor_copy(g.tile_expert[:], experts_f[:]))
            dve.wait_ge(found_ready, 1)
            then(nc.vector.tensor_scalar(vacant[:], found_ps[:, 0:SG], 0.0, float(T + P), ALU.is_equal, ALU.mult))
            then(nc.vector.scalar_tensor_tensor(vacant[:], found_ps[:, 0:SG], float(P), vacant[:], ALU.mult, ALU.add))
            then(nc.vector.scalar_tensor_tensor(found[:], found_ps[:, SG:2 * SG], -float(P), vacant[:], ALU.add, ALU.add))
            then(nc.vector.tensor_copy(g.slot_token[:], found[:]))


def experts(nc, g):
    with ExitStack() as ctx:
        sb = lambda name, shape, dt=F32: ctx.enter_context(nc.sbuf_tensor(name, shape, dt))
        sem = lambda name: ctx.enter_context(nc.semaphore(name))
        NC = len(CHUNKS)
        w_top, w_tail, w3 = sb("w_top", [P, S, 2, F]), sb("w_tail", [P, S, F]), sb("w3", [FC, S, NC, D])
        rows = g.slot_rows
        numbers, out_numbers = sb("numbers", [P, S], U32), sb("out_numbers", [P, S], U32)
        tt = sb("slot_t", [P, S, 2 * FT])
        act_sb = sb("silu", [FC, 2, FT])
        hid = sb("hidden", [FC, S, NC, FT])
        y = sb("y", [P, S, D])
        psum = lambda name, shape: ctx.enter_context(nc.psum_tensor(name, shape, F32))
        t_ps = psum("slot_ps", [P, 2 * FT])
        h_ps = [[psum(f"hid{h}_ps{i}", [FC, HALF]) for h in range(2)] for i in range(3)]
        y_ps = psum("y_ps", [P, HALF])

        top_taken, tail_taken = sem("top_taken"), sem("tail_taken")
        rows_loaded = [sem(f"rows_loaded{j}") for j in range(S)]
        t_ready, t_copied = sem("slot_t_ready"), sem("slot_t_copied")
        h_ready, silu_done, hid_done = sem("h_ready"), sem("silu_done"), sem("hid_done")
        y_ready, y_added = sem("y_ready"), sem("y_added")
        turn, numbered, out_numbered = sem("turn"), sem("numbered"), sem("out_numbered")
        y_stored = [sem(f"y_stored{j}") for j in range(S)]
        block = ctx.enter_context(nc.Block())
        N_T = FFN_TILES

        @block.gpsimd
        def _(pool):
            last_row = pool.to_reg(T - 1)

            def fetch(n, j):
                nc.gpsimd.tensor_copy(numbers[:, j:j + 1], g.slot_token[:, bass.ds(n, 1)]).then_inc(numbered, 1)
                pool.wait_ge(numbered, n + 1)
                pool.sem_inc(turn, 1)
                pool.indirect_dma_start(rows[:, j, :], None, g.token_rows, bass.IndirectOffsetOnAxis(ap=numbers[:, j:j + 1], axis=0),
                                        bounds_check=last_row, oob_is_err=False).then_inc(rows_loaded[j], 16)

            for n in range(S - 1):
                fetch(n, n)

            def step(s):
                j = s.slot
                if s.after(S - 1):
                    fetch(s.n + S - 1, (j - 1) % S)
                if s.before(S):
                    pool.wait_ge(y_stored[j], 16 * s.group)
                    pool.sem_inc(turn, 1)
                nc.gpsimd.tensor_copy(out_numbers[:, j:j + 1], g.slot_token[:, bass.ds(s.n, 1)]).then_inc(out_numbered, 1)
                pool.wait_ge(out_numbered, s.n + 1)
                pool.wait_ge(y_added, s.n + 1)
                pool.sem_inc(turn, 1)
                pool.indirect_dma_start(g.out_rows, bass.IndirectOffsetOnAxis(ap=out_numbers[:, j:j + 1], axis=0),
                                        y[:, j, :], None, bounds_check=last_row, oob_is_err=False).then_inc(y_stored[j], 16)

            steps(pool, N_T, S, step)
            for j in range(S):
                pool.wait_ge(y_stored[j], 16 * ((N_T - j + S - 1) // S))

        @block.tensor
        def _(pe):
            def transposes(n, group, j, reused):
                pe.wait_ge(rows_loaded[j], 16 * (group + 1))
                if reused:
                    pe.wait_ge(t_copied, n)
                for c in range(2):
                    last = nc.tensor.transpose(t_ps[:, c * FT:(c + 1) * FT], rows[:, j, c * P:(c + 1) * P], g.ident[:])
                last.then_inc(t_ready, 1)

            def hidden(s, k):
                j = s.slot
                at, size = CHUNKS[k]
                if s.before(1) or k >= 3:
                    pe.wait_ge(hid_done, NC * s.n + k - 2)
                out = h_ps[(j + k) % 3]
                for h in range(2):
                    nc.tensor.matmul(out[h][0:size, 0:FT], w_top[:, j, h, at:at + size], tt[:, j, 0:FT], start=True, stop=False)
                for h in range(2):
                    half = slice(h * TAIL, (h + 1) * TAIL)
                    last = nc.tensor.matmul(out[h][0:size, 0:FT], w_tail[half, j, at:at + size], tt[half, j, FT:2 * FT],
                                            start=False, stop=True, tile_position=(h * TAIL, 0))
                last.then_inc(h_ready, 1)

            def output(n, j, reused):
                if reused:
                    pe.wait_ge(y_added, n)
                for k, (at, size) in enumerate(CHUNKS):
                    pe.wait_ge(hid_done, NC * n + k + 1)
                for k, (at, size) in enumerate(CHUNKS):
                    last = nc.tensor.matmul(y_ps[:, 0:D], hid[0:size, j, k, :], w3[0:size, j, k, :], start=(k == 0), stop=(k == NC - 1))
                last.then_inc(y_ready, 1)

            transposes(0, 0, 0, False)

            def step(s):
                j = s.slot
                pe.wait_ge(top_taken, s.n + 1)
                pe.wait_ge(tail_taken, 3 * s.n + 3)
                pe.wait_ge(t_copied, s.n + 1)
                hidden(s, 0)
                if s.before(1):
                    output(s.n - 1, (j - 1) % S, s.before(2))
                for k in range(1, NC):
                    hidden(s, k)
                    if k == 1 and s.after(1):
                        transposes(s.n + 1, s.group + (j + 1) // S, (j + 1) % S, True)

            steps(pe, N_T, S, step)
            output(N_T - 1, (N_T - 1) % S, True)

        @block.scalar
        def _(act):
            def copy_t(n, j, reused):
                act.wait_ge(t_ready, n + 1)
                if reused:
                    act.wait_ge(h_ready, NC * (n - S + 1))
                nc.scalar.activation(tt[:, j, :], t_ps[:], ACT.Copy).then_inc(t_copied, 1)

            def take_top(n, j, reused):
                e = act.value_load(g.tile_expert[0:1, bass.ds(n, 1)], min_val=0, max_val=EXPERTS - 1)
                if reused:
                    act.wait_ge(h_ready, NC * (n - S + 1))
                nc.scalar.activation(w_top[:, j].rearrange("p h f -> p (h f)"), g.w_top[:, bass.ds(e, 1)].rearrange("p e h f -> p (e h f)"),
                                     ACT.Copy).then_inc(top_taken, 1)

            take_top(0, 0, False)
            copy_t(0, 0, False)
            take_top(1, 1, False)

            def step(s):
                for k, (at, size) in enumerate(CHUNKS):
                    act.wait_ge(h_ready, NC * s.n + k + 1)
                    if s.before(1) or k >= 2:
                        act.wait_ge(hid_done, NC * s.n + k - 1)
                    nc.scalar.activation(act_sb[0:size, k % 2, :], h_ps[(s.slot + k) % 3][0][0:size, 0:FT], ACT.Silu).then_inc(silu_done, 1)
                    if k == 1 and s.after(1):
                        copy_t(s.n + 1, (s.slot + 1) % S, s.before(2))
                if s.after(2):
                    take_top(s.n + 2, (s.slot + 2) % S, s.before(1))

            steps(act, N_T, S, step)

        @block.vector
        def _(dve):
            def add_residual(n, j, stores):
                dve.wait_ge(y_ready, n + 1)
                if stores is not None:
                    dve.wait_ge(y_stored[j], 16 * stores)
                nc.vector.tensor_tensor(y[:, j], y_ps[:, 0:D], rows[:, j, AT_X:ROW], ALU.add).then_inc(y_added, 1)

            def take_tail(n, j):
                e = dve.value_load(g.tile_expert[0:1, bass.ds(n, 1)], min_val=0, max_val=EXPERTS - 1)
                left = F - (NC - 1) * FC
                nc.vector.tensor_copy(w_tail[:, j:j + 1, :], g.w_tail[:, bass.ds(e, 1), :]).then_inc(tail_taken, 1)
                nc.vector.tensor_copy(w3[:, j:j + 1, 0:NC - 1, :], g.w3[:, bass.ds(e, 1), 0:NC - 1, :]).then_inc(tail_taken, 1)
                nc.vector.tensor_copy(w3[0:left, j:j + 1, NC - 1, :], g.w3[0:left, bass.ds(e, 1), NC - 1, :]).then_inc(tail_taken, 1)

            take_tail(0, 0)
            take_tail(1, 1)

            def step(s):
                for k, (at, size) in enumerate(CHUNKS):
                    dve.wait_ge(silu_done, NC * s.n + k + 1)
                    if s.before(S):
                        dve.wait_ge(y_ready, s.n - S + 1)
                    nc.vector.tensor_tensor(hid[0:size, s.slot, k, :], h_ps[(s.slot + k) % 3][1][0:size, 0:FT], act_sb[0:size, k % 2, :], ALU.mult).then_inc(hid_done, 1)
                    if k == 0 and s.before(1):
                        back = (s.slot - 1) % S
                        add_residual(s.n - 1, back, (s.group - (s.slot == 0)) if s.before(S + 1) else None)
                if s.after(2):
                    take_tail(s.n + 2, (s.slot + 2) % S)

            steps(dve, N_T, S, step)
            add_residual(N_T - 1, (N_T - 1) % S, (N_T - 1) // S)


def key_rows():
    import numpy as np
    r = np.arange(HS)
    tile, row, col = np.meshgrid(np.arange(KT), np.arange(P // HS), np.arange(HS), indexing="ij")
    row = (tile % 2 * (P // HS) + row).reshape(1, N)
    col = col.reshape(1, N)
    hot = np.concatenate([row == r[:, None], col == r[:, None]])
    return np.concatenate([hot, hot, np.ones((1, N), bool)]).astype(np.float16)


def constants():
    import numpy as np
    f = np.float32
    E = EXPERTS
    every = lambda a: np.ascontiguousarray(np.broadcast_to(a.astype(f), (P,) + a.shape))
    return {
        "ident": np.eye(P, dtype=f),
        "low_rows": (np.arange(4 * HD) // HD % 2).astype(f)[:, None],
        "key_rows": key_rows(),
        "fold": np.tile(np.eye(4 * HD, dtype=f), (2, 1)),
        "tri": np.triu(np.ones((P, P), np.float16), 1),
        "ones": np.ones((P, P), np.float16),
        "expert": every(np.repeat(np.arange(E)[:, None], TT, 1)),
        "run": every(np.repeat(np.arange(TT)[None] > 0, E, 0)),
        "fills": every(np.repeat(np.arange(T // FT)[None] * FT, E, 0)),
        "tile_no": every(np.repeat(np.arange(FFN_TILES)[:, None], E, 1)),
        "tile": every(1 + np.arange(TT)),
        "lane_of": np.arange(P).astype(f)[:, None],
        "group_no": every(np.repeat(np.arange(SG)[None], TT, 0)),
        "lane_no": every(np.arange(P)),
    }


def build(nc, ins, out):
    g = Shared()
    g.ident_dram, g.low_rows_dram, g.key_rows_dram, g.fold_dram = ins["ident"], ins["low_rows"], ins["key_rows"], ins["fold"]
    g.route_dram = {name: ins[name] for name in ROUTE_TABLES}
    g.x_tiles = ins["x"].rearrange("(t p) d -> p t d", p=P)
    g.qkv_wt, g.qkv_b, g.rel_tables = ins["qkv_wt"], ins["qkv_b"], [ins["rel_h"], ins["rel_w"]]
    g.proj_wt, g.proj_b, g.gate_wt, g.gate_b = ins["proj_wt"], ins["proj_b"], ins["gate_wt"], ins["gate_b"]
    g.w1_t, g.w2_t, g.w3_t = ins["w1_t"], ins["w2_t"], ins["w3_t"]
    g.out_rows = out
    g.qk_split = nc.dram_tensor("qk_split", [2, 2, B * D, N], F16, kind="Internal").ap()
    g.qk_heads = g.qk_split.rearrange("k s (b h r) n -> k s h r b n", b=B, h=HEADS)
    g.rel_split = nc.dram_tensor("rel_split", [2, 2, HEADS, B, H, N], F16, kind="Internal").ap()
    g.rel_pairs = g.rel_split.rearrange("a s h b r n -> a s (h b) r n")
    g.token_rows = nc.dram_tensor("token_rows", [T, ROW], F32, kind="Internal").ap()
    g.token_tiles = g.token_rows.rearrange("(t p) d -> p t d", p=P)
    with ExitStack() as ctx:
        sb = lambda name, shape, dt=F32: ctx.enter_context(nc.sbuf_tensor(name, shape, dt))
        g.ident = sb("ident_sb", [P, P])
        g.x_sb = sb("x_sb", [P, TT, D])
        g.att_sb = sb("att_sb", [P, BH, KT, HD])
        g.gates = sb("gates_sb", [P, TT, EXPERTS])
        g.tile_expert = sb("tile_expert", [P, FFN_TILES], I32)
        g.slot_token = sb("slot_token", [P, FFN_TILES], U32)
        g.slot_rows = sb("slot_rows", [P, S, ROW])
        g.route_tables = {name: sb(name + "_sb", shape, F16 if name in ("tri", "ones") else F32) for name, shape in ROUTE_TABLES.items()}
        with ExitStack() as attention_ctx:
            sb = lambda name, shape, dt=F32: attention_ctx.enter_context(nc.sbuf_tensor(name, shape, dt))
            g.table = sb("table", [4 * HD, 2 * (2 * H - 1)])
            g.low_rows = sb("low_rows", [4 * HD, 1])
            g.v_sb = sb("v_sb", [P, BH, KT, VW])
            rows = 3 * HD + 4 * HS + 1
            g.q_side = [sb(f"q_side{j}", [rows, 4, N], F16) for j in range(B)]
            g.k_side = [sb(f"k_side{j}", [rows, N], F16) for j in range(B)]
            g.fold = sb("fold_sb", [P, 4 * HD])
            g.loaded = [attention_ctx.enter_context(nc.semaphore(f"loaded{j}")) for j in range(B)]
            g.att_consts_loaded = attention_ctx.enter_context(nc.semaphore("att_consts_loaded"))
            project(nc, g)
            relative_positions(nc, g)
            attention(nc, g)
        sb = lambda name, shape, dt=F32: ctx.enter_context(nc.sbuf_tensor(name, shape, dt))
        g.w_top, g.w_tail = sb("w_top_all", [P, EXPERTS, 2, F]), sb("w_tail_all", [P, EXPERTS, F])
        g.w3 = sb("w3_all", [FC, EXPERTS, len(CHUNKS), D])
        gate(nc, g)
        route(nc, g)
        experts(nc, g)


def kernel(x, L0_conv_qkv_w, L0_conv_qkv_b, L0_conv_proj_w, L0_conv_proj_b, L0_conv_rel_pos_h, L0_conv_rel_pos_w,
           L0_ffn_Wg, L0_ffn_bg, L0_ffn_W1, L0_ffn_W2, L0_ffn_W3):
    import numpy as np
    import concourse.bacc as bacc
    from concourse.bass_utils import run_bass_kernel_spmd

    turned = lambda a: np.ascontiguousarray(np.swapaxes(np.asarray(a), -1, -2))
    row = lambda a: np.asarray(a).reshape(1, -1)
    arrays = {
        "x": np.asarray(x).reshape(T, D),
        "qkv_wt": turned(L0_conv_qkv_w), "qkv_b": row(L0_conv_qkv_b),
        "proj_wt": turned(L0_conv_proj_w), "proj_b": row(L0_conv_proj_b),
        "rel_h": turned(np.asarray(L0_conv_rel_pos_h)[::-1]), "rel_w": turned(np.asarray(L0_conv_rel_pos_w)[::-1]),
        "gate_wt": turned(L0_ffn_Wg), "gate_b": row(L0_ffn_bg),
        "w1_t": turned(L0_ffn_W1), "w2_t": turned(L0_ffn_W2), "w3_t": turned(L0_ffn_W3),
        **constants(),
    }
    nc = bacc.Bacc("TRN2", target_bir_lowering=False, num_devices=1)
    ins = {name: nc.dram_tensor(f"in_{name}", a.shape, mybir.dt.from_np(a.dtype), kind="ExternalInput").ap()
           for name, a in arrays.items()}
    out = nc.dram_tensor("out", [T, D], F32, kind="ExternalOutput").ap()
    build(nc, ins, out)
    result = run_bass_kernel_spmd(nc, [{f"in_{name}": a for name, a in arrays.items()}], core_ids=[0])
    return result.results[0]["out"].reshape(B, H, W, D)
```
